# Optimizing a Trainium2 kernel written in Bass

```python
import numpy as np
import jax
import jax.numpy as jnp

def _softmax(x, axis=-1):
    return jax.nn.softmax(x, axis=axis)

def _gelu(x):
    return jax.nn.gelu(x, approximate=True)

def _silu(x):
    return jax.nn.silu(x)

def _sigmoid(x):
    return jax.nn.sigmoid(x)

def _layernorm(x, axis=-1, eps=1e-05):
    m = jnp.mean(x, axis=axis, keepdims=True)
    v = jnp.var(x, axis=axis, keepdims=True)
    return (x - m) / jnp.sqrt(v + eps)

def _scatter_add(tgt, idx, src, axis=0):
    return tgt.at[idx].add(src)

def _segment_sum(src, seg, n):
    return jax.ops.segment_sum(src, seg, n)
kernel_name = 'mk_cond_resid_d2_seqx_r8_e40bfb'

def setup_inputs(seed: int=0):
    np.random.seed(seed)
    _w = jnp.asarray

    def _rec_inputs():
        import jax
        import jax.numpy as jnp
        _rk = jax.random.key(seed)
        x = -0.0002928 + 1 * jax.random.normal(jax.random.fold_in(_rk, 1), (8, 256, 128), jnp.float32)
        _lenS = 256 - jax.random.randint(jax.random.fold_in(_rk, 7), (8,), 0, max(1, 256 // 4) + 1, jnp.int32)
        _lenS2 = 256 - jax.random.randint(jax.random.fold_in(_rk, 8), (8,), 0, max(1, 256 // 4) + 1, jnp.int32)
        cond_256 = -0.106481 + 1.03144 * jax.random.normal(jax.random.fold_in(_rk, 11), (8, 32), jnp.float32)
        return (x, cond_256)
    x, cond_256 = _rec_inputs()

    def _L0_cond_setup():
        import jax, jax.numpy as jnp
        import numpy as np
        TOP_K = 2
        EPS = 1e-06
        B, S, H, G, E, M = (2, 256, 128, 32, 8, 256)
        key = jax.random.key(seed)
        ks = jax.random.split(key, 16)
        s_h = 1.0 / np.sqrt(H)
        s_g = 1.0 / np.sqrt(G)
        s_m = 1.0 / np.sqrt(M)
        return {'x': jax.random.normal(ks[0], (B, S, H), jnp.float32), 'genre_embed': jax.random.normal(ks[1], (B, 1, G), jnp.float32), 'rms_w': jnp.ones((H,), jnp.float32), 'wg_W': jax.random.normal(ks[2], (H, E), jnp.float32) * s_h, 'wg_b': jnp.zeros((E,), jnp.float32), 'gg_W': jax.random.normal(ks[3], (G, E), jnp.float32) * s_g, 'gg_b': jnp.zeros((E,), jnp.float32), 'W1': jax.random.normal(ks[4], (E, H, M), jnp.float32) * s_h, 'b1': jnp.zeros((E, M), jnp.float32), 'W2': jax.random.normal(ks[5], (E, M, M), jnp.float32) * s_m, 'b2': jnp.zeros((E, M), jnp.float32), 'W3': jax.random.normal(ks[6], (E, M, H), jnp.float32) * s_m, 'b3': jnp.zeros((E, H), jnp.float32)}
    _L0_cond_all = _L0_cond_setup()
    _L0_cond_in = {k: v for k, v in _L0_cond_all.items() if k in ('rms_w', 'wg_W', 'wg_b', 'gg_W', 'gg_b', 'W1', 'b1', 'W2', 'b2', 'W3', 'b3')}
    del _L0_cond_all

    def _L1_cond_setup():
        import jax, jax.numpy as jnp
        import numpy as np
        EPS = 1e-08

        def hamilton(q1, q2):
            w1, x1, y1, z1 = (q1[..., i, :] for i in range(4))
            w2, x2, y2, z2 = (q2[..., i, :] for i in range(4))
            w = w1 * w2 - x1 * x2 - y1 * y2 - z1 * z2
            x = w1 * x2 + x1 * w2 + y1 * z2 - z1 * y2
            y = w1 * y2 - x1 * z2 + y1 * w2 + z1 * x2
            z = w1 * z2 + x1 * y2 - y1 * x2 + z1 * w2
            return jnp.stack([w, x, y, z], axis=-2)

        def _normalize(q):
            return q / jnp.sqrt(jnp.sum(q * q, axis=0, keepdims=True) + EPS)
        key = jax.random.key(seed)
        k1, k2, k3, k4 = jax.random.split(key, 4)
        B, T, d_model = (4, 512, 128)
        quat_dim = d_model // 4
        x = jax.random.normal(k1, (B, T, d_model), dtype=jnp.float32)
        q_left = jax.random.normal(k2, (4, quat_dim), dtype=jnp.float32)
        q_right = jax.random.normal(k3, (4, quat_dim), dtype=jnp.float32)
        spectral_gate = jax.random.uniform(k4, (1, 1, 1, quat_dim), dtype=jnp.float32)
        return {'x': x, 'q_left': q_left, 'q_right': q_right, 'spectral_gate': spectral_gate}
    _L1_cond_all = _L1_cond_setup()
    _L1_cond_in = {k: v for k, v in _L1_cond_all.items() if k in ('q_right', 'spectral_gate')}
    del _L1_cond_all
    return {'x': x, 'cond_256': cond_256, 'L0_cond_rms_w': _L0_cond_in['rms_w'], 'L0_cond_wg_W': _L0_cond_in['wg_W'], 'L0_cond_wg_b': _L0_cond_in['wg_b'], 'L0_cond_gg_W': _L0_cond_in['gg_W'], 'L0_cond_gg_b': _L0_cond_in['gg_b'], 'L0_cond_W1': _L0_cond_in['W1'], 'L0_cond_b1': _L0_cond_in['b1'], 'L0_cond_W2': _L0_cond_in['W2'], 'L0_cond_b2': _L0_cond_in['b2'], 'L0_cond_W3': _L0_cond_in['W3'], 'L0_cond_b3': _L0_cond_in['b3'], 'L1_cond_q_right': _L1_cond_in['q_right'], 'L1_cond_spectral_gate': _L1_cond_in['spectral_gate']}

def reference(x, cond_256, L0_cond_rms_w, L0_cond_wg_W, L0_cond_wg_b, L0_cond_gg_W, L0_cond_gg_b, L0_cond_W1, L0_cond_b1, L0_cond_W2, L0_cond_b2, L0_cond_W3, L0_cond_b3, L1_cond_q_right, L1_cond_spectral_gate):
    import jax
    import jax.numpy as jnp

    def _L0_cond_ref(x, genre_embed, rms_w, wg_W, wg_b, gg_W, gg_b, W1, b1, W2, b2, W3, b3):
        import jax, jax.numpy as jnp
        import numpy as np
        TOP_K = 2
        EPS = 1e-06
        E = W1.shape[0]
        var = jnp.mean(x * x, axis=-1, keepdims=True)
        xn = rms_w * (x * jax.lax.rsqrt(var + EPS))
        gate = xn @ wg_W + wg_b + (genre_embed @ gg_W + gg_b)
        gate_w = jax.nn.softmax(gate, axis=-1)
        topk_w, topk_i = jax.lax.top_k(gate_w, TOP_K)
        cw = jnp.sum(jax.nn.one_hot(topk_i, E, dtype=x.dtype) * topk_w[..., None], axis=-2)
        h1 = jax.nn.relu(jnp.einsum('bsh,ehm->bsem', x, W1) + b1)
        h2 = jax.nn.relu(jnp.einsum('bsem,emn->bsen', h1, W2) + b2)
        out_e = jnp.einsum('bsen,enh->bseh', h2, W3) + b3
        return jnp.einsum('bseh,bse->bsh', out_e, cw)

    def _L1_cond_ref(x, q_left, q_right, spectral_gate):
        import jax, jax.numpy as jnp
        import numpy as np
        EPS = 1e-08

        def hamilton(q1, q2):
            w1, x1, y1, z1 = (q1[..., i, :] for i in range(4))
            w2, x2, y2, z2 = (q2[..., i, :] for i in range(4))
            w = w1 * w2 - x1 * x2 - y1 * y2 - z1 * z2
            x = w1 * x2 + x1 * w2 + y1 * z2 - z1 * y2
            y = w1 * y2 - x1 * z2 + y1 * w2 + z1 * x2
            z = w1 * z2 + x1 * y2 - y1 * x2 + z1 * w2
            return jnp.stack([w, x, y, z], axis=-2)

        def _normalize(q):
            return q / jnp.sqrt(jnp.sum(q * q, axis=0, keepdims=True) + EPS)
        B, T, d_model = x.shape
        quat_dim = d_model // 4
        x_quat = x.reshape(B, T, 4, quat_dim)
        x_spectral = jnp.fft.fft(x_quat, axis=1)
        x_filtered = jnp.fft.ifft(x_spectral * spectral_gate, axis=1).real.astype(x.dtype)
        q_left_n = _normalize(q_left)
        q_right_n = _normalize(q_right)
        conj_sign = jnp.array([1.0, -1.0, -1.0, -1.0], dtype=x.dtype)[:, None]
        q_right_conj = q_right_n * conj_sign
        x_right = hamilton(x_filtered, q_right_conj)
        x_rotated = hamilton(q_left_n, x_right)
        return x_rotated.reshape(B, T, d_model)
    x = x + _L0_cond_ref(x, cond_256[:, None, :], L0_cond_rms_w, L0_cond_wg_W, L0_cond_wg_b, L0_cond_gg_W, L0_cond_gg_b, L0_cond_W1, L0_cond_b1, L0_cond_W2, L0_cond_b2, L0_cond_W3, L0_cond_b3)
    x = x + _L1_cond_ref(x, cond_256, L1_cond_q_right, L1_cond_spectral_gate)
    return x

_drawn_inputs = setup_inputs


def setup_inputs(seed=0):
    import zlib

    import numpy as np

    out = dict(_drawn_inputs(seed))
    spreads = {'L0_cond_rms_w': (1.0, 0.2),
     'L0_cond_wg_b': (0.0, 0.1),
     'L0_cond_gg_b': (0.0, 0.1),
     'L0_cond_b1': (0.0, 0.318),
     'L0_cond_b2': (0.0, 0.1),
     'L0_cond_b3': (0.0, 0.1)}
    factors = {}
    for name, (base, spread) in spreads.items():
        noise = np.random.default_rng([zlib.crc32(name.encode()), seed]).standard_normal(out[name].shape)
        drawn = base * np.exp(spread * noise) if base else spread * noise
        out[name] = jnp.asarray(drawn.astype(out[name].dtype))
    for name, factor in factors.items():
        out[name] = (out[name] * factor).astype(out[name].dtype)
    return out
```

```python
from contextlib import ExitStack

import concourse.bass as bass
from concourse import mybir

F32 = mybir.dt.float32
F16 = mybir.dt.float16
I32 = mybir.dt.int32
ALU = mybir.AluOpType
ACT = mybir.ActivationFunctionType
X_AXIS = mybir.AxisListType.X

P = 128
BATCH, SEQ, H = 8, 256, 128
TOKENS = BATCH * SEQ
COLS = TOKENS // P
E, M, G = 8, 256, 32
TOP_K = 2
PAIRS = TOP_K * COLS
MC = M // P
UNROLL = 3
NUM_TILES = (TOP_K * TOKENS + E * (P - 1)) // P
TABLE = NUM_TILES + UNROLL
QUAT = 4
QD = H // QUAT
CHUNKS = 4
CPC = COLS // CHUNKS
EPS_RMS = 1e-6
EPS_QUAT = 1e-8

LEFT = [[(0, 1), (1, -1), (2, -1), (3, -1)],
        [(1, 1), (0, 1), (3, -1), (2, 1)],
        [(2, 1), (3, 1), (0, 1), (1, -1)],
        [(3, 1), (2, -1), (1, 1), (0, 1)]]
RIGHT_CONJ = [[(0, 1), (1, 1), (2, 1), (3, 1)],
              [(1, -1), (0, 1), (3, -1), (2, 1)],
              [(2, -1), (3, 1), (0, 1), (1, -1)],
              [(3, -1), (2, -1), (1, 1), (0, 1)]]

FIRST_STEADY = 4
LAST_STEP = NUM_TILES
STEADY_TRIPS = (NUM_TILES - 2 - FIRST_STEADY) // UNROLL
PEEL_AFTER = FIRST_STEADY + STEADY_TRIPS * UNROLL

ROW = 4
LIVE = UNROLL + 2
EARLY_ROWS = 3
ROWS = (FIRST_STEADY + 2) // UNROLL + STEADY_TRIPS + 1


def wait_count(engine, semaphore, count):
    if isinstance(count, int) and count <= 0:
        return
    engine.wait_ge(semaphore, count)


def moe_rotation(nc, x, cond, rms_w, wg_w, wg_b, gg_w, gg_b, w1, b1, w2, b2, w3, b3,
                 q_right, gate, out):
    y_rows = nc.dram_tensor("y_rows", (TOP_K * TOKENS + TABLE * P, H), F32, kind="Internal").ap()

    with ExitStack() as ctx:
        def sb(name, shape, dt=F32):
            return ctx.enter_context(nc.sbuf_tensor(name, shape, dt))

        def ps(name, shape):
            return ctx.enter_context(nc.psum_tensor(name, shape, F32))

        def sem(name):
            return ctx.enter_context(nc.semaphore(name))

        x_sb = sb("x_sb", [P, COLS, H])
        w1_sb = sb("w1_sb", [P, E, M])
        w2_sb = sb("w2_sb", [P, E, MC, M])
        w3_sb = sb("w3_sb", [P, E * MC, H])
        b1_rows = sb("b1_rows", [P, E, M])
        b2_rows = sb("b2_rows", [P, E, M])
        b3_sb = sb("b3_sb", [E, H])
        rms_sb = sb("rms_sb", [H, 1])
        wg_sb = sb("wg_sb", [H, E])
        wg_b_sb = sb("wg_b_sb", [1, E])
        gg_b_sb = sb("gg_b_sb", [1, E])
        gg_sb = sb("gg_sb", [G, E])
        cond_t = sb("cond_t", [G, BATCH])
        qr_t = sb("qr_t", [QD, QUAT])
        gate_t = sb("gate_t", [QD, 1])

        ident = sb("ident", [P, P])
        before = sb("before", [P, P], F16)
        ones16 = sb("ones16", [P, P], F16)
        ones_row = sb("ones_row", [1, P])
        lane_i = sb("lane_i", [P, P], I32)
        lane16 = sb("lane16", [P, P], F16)
        rev_e_i = sb("rev_e_i", [P, E], I32)
        rev_e = sb("rev_e", [P, E])
        thresh_i = sb("thresh_i", [P, COLS], I32)
        thresh = sb("thresh", [P, COLS])
        token1_i = sb("token1_i", [P, COLS], I32)
        token1 = sb("token1", [P, COLS])
        spare_i = sb("spare_i", [P, TABLE], I32)
        spare = sb("spare", [P, TABLE])
        tiles_i = sb("tiles_i", [1, ROWS, ROW], I32)
        tiles_f = sb("tiles_f", [1, ROWS, ROW])
        zeros_e = sb("zeros_e", [P, E])

        x_sq = sb("x_sq", [P, COLS, H])
        x_t = sb("x_t", [H, COLS, P])
        wg_rms = sb("wg_rms", [H, E])
        bias_row = sb("bias_row", [1, E])
        cond_rep = sb("cond_rep", [G, BATCH, COLS])
        var = sb("var", [P, COLS])
        rms = sb("rms", [P, COLS])
        rstd = sb("rstd", [P, COLS])
        logits = sb("logits", [P, COLS, E])
        row_max = sb("row_max", [P, COLS])
        expv = sb("expv", [P, COLS, E])
        row_sum = sb("row_sum", [P, COLS])
        probs = sb("probs", [P, COLS, E])
        weight = sb("weight", [P, TOP_K, COLS])
        key = sb("key", [P, COLS, E])
        key_max = sb("key_max", [P, COLS])
        chosen = sb("chosen", [P, TOP_K, COLS, E])
        pick = [sb(f"pick{n}", [P, 2 * COLS, E], F16) for n in range(2)]
        pick_one = sb("pick_one", [P, COLS, E], F16)
        over = sb("over", [P, E, COLS])
        tile_count = sb("tile_count", [P, E])
        tile_end = sb("tile_end", [P, E])
        tile_start = sb("tile_start", [P, E])
        position = sb("position", [P, COLS, E])
        pos_chosen = sb("pos_chosen", [P, TOP_K, COLS, E])
        slot = sb("slot", [P, PAIRS])
        slot_i = sb("slot_i", [P, PAIRS], I32)
        lane_of_i = sb("lane_of_i", [P, PAIRS], I32)
        tile_of_i = sb("tile_of_i", [P, PAIRS], I32)
        lane_of = sb("lane_of", [P, PAIRS])
        tile_of = sb("tile_of", [P, PAIRS])
        lane_hot = sb("lane_hot", [P, PAIRS, P], F16)
        tile_hot = sb("tile_hot", [P, PAIRS, TABLE], F16)
        second = sb("second", [P, TABLE])
        filled = sb("filled", [P, TABLE])
        is_second = sb("is_second", [P, TABLE])
        is_unused = sb("is_unused", [P, TABLE])
        row_1 = sb("row_1", [P, TABLE])
        gather_f = sb("gather_f", [P, TABLE])
        gather_row = sb("gather_row", [P, TABLE], I32)
        scatter_row = sb("scatter_row", [P, TABLE], I32)
        ended = sb("ended", [1, ROWS * ROW, E])
        expert_f = sb("expert_f", [1, ROWS * ROW])
        tile_expert = sb("tile_expert", [1, ROWS, ROW], I32)

        q_sq = sb("q_sq", [QD, BATCH + QUAT])
        q_norm = sb("q_norm", [QD, 2])
        q_root = sb("q_root", [QD, 2])
        q_inv = sb("q_inv", [QD, 2])
        ql_n = sb("ql_n", [QD, QUAT])
        qr_n = sb("qr_n", [QD, QUAT])
        left = sb("left", [QD, QUAT, QUAT])
        right_t = sb("right_t", [QD, QUAT, QUAT])
        lr_prod = sb("lr_prod", [QD, QUAT, QUAT, QUAT])
        coef = sb("coef", [QD, QUAT, QUAT])
        rot0 = sb("rot0", [H, H])
        rot = sb("rot", [H, H])
        w3_t = sb("w3_t", [H, E * MC, P])
        w3_rot = sb("w3_rot", [P, E * MC, H])
        b3_t = sb("b3_t", [H, E])
        b3_cols = sb("b3_cols", [H, E, P])
        b3_rows = sb("b3_rows", [P, E, H])
        base = sb("base", [P, COLS, H])

        x_g = sb("x_g", [P, UNROLL, H])
        gather_idx = sb("gather_idx", [P, UNROLL], I32)
        scatter_idx = sb("scatter_idx", [P, UNROLL], I32)
        x_gt = sb("x_gt", [H, P])
        h1 = sb("h1", [P, M])
        h1_t = sb("h1_t", [P, MC, P])
        h2 = sb("h2", [P, M])
        h2_t = sb("h2_t", [P, MC, P])
        y = sb("y", [P, UNROLL, H])
        y_back = sb("y_back", [P, TOP_K, COLS, H])
        partial = sb("partial", [P, COLS, H])
        out_sb = sb("out_sb", [P, COLS, H])

        bank = [ps(f"bank{n}", [P, 512]) for n in range(8)]

        s_x = [sem(f"x_loaded{g}") for g in range(CHUNKS)]
        s_small = sem("small_loaded")
        s_w1, s_w2, s_w3 = sem("w1_loaded"), sem("w2_loaded"), sem("w3_loaded")
        s_b1, s_b2 = sem("b1_loaded"), sem("b2_loaded")
        s_const = sem("constants_made")
        s_pool = sem("pool_steps")
        s_coefs = sem("quaternion_signs_placed")
        s_sq = sem("x_squared")
        s_tr = sem("x_transposed")
        s_xt = sem("x_t_copied")
        s_wgr = sem("wg_rms_made")
        s_bias = sem("gate_bias_done")
        s_logit = sem("logits_done")
        s_var, s_rms, s_qn, s_qroot = sem("var_made"), sem("rms_made"), sem("q_norm_made"), sem("q_root_made")
        s_shift, s_exp = sem("logits_shifted"), sem("exp_made")
        s_qhat = sem("q_normalized")
        s_pick = sem("picks_made")
        s_rank = sem("ranks_done")
        s_dve = sem("router_steps")
        s_hot = sem("one_hots_made")
        s_inv = sem("slots_inverted")
        s_tables = sem("tables_made")
        s_rot = sem("rotation_made")
        s_w3tp, s_w3t = sem("w3_transposed"), sem("w3_t_copied")
        s_w3rp, s_w3r = sem("w3_rotated"), sem("w3_rot_copied")
        s_b3tp, s_b3t, s_b3rp, s_b3r = sem("b3_transposed"), sem("b3_spread"), sem("b3_rotated"), sem("b3_rows_copied")
        s_xrp, s_base = sem("x_rotated"), sem("base_copied")
        s_gidx = sem("gather_index_set")
        s_go = sem("pool_dma_allowed")
        s_gather = [sem(f"gathered{n}") for n in range(UNROLL)]
        s_t0, s_xgt = sem("tile_transposed"), sem("tile_t_copied")
        s_l1, s_h1, s_t1, s_h1t = sem("layer1_done"), sem("h1_biased"), sem("h1_transposed"), sem("h1_t_ready")
        s_l2, s_h2, s_t2, s_h2t = sem("layer2_done"), sem("h2_biased"), sem("h2_transposed"), sem("h2_t_ready")
        s_l3, s_y = sem("layer3_done"), sem("y_ready")
        s_scatter = [sem(f"scattered{n}") for n in range(UNROLL)]
        s_back = [sem(f"y_loaded{g}") for g in range(CHUNKS)]
        s_partial, s_out, s_store = sem("partial_made"), sem("out_made"), sem("stored")
        NUM_SMALL = 9

        block = ctx.enter_context(nc.Block())

        x_rows = x.rearrange("b s h -> (b s) h")
        x_pc = x_rows.rearrange("(p c) h -> p c h", c=COLS)
        out_pc = out.rearrange("b s h -> (b s) h").rearrange("(p c) h -> p c h", c=COLS)

        def chunk(g):
            return slice(g * CPC, (g + 1) * CPC)

        @block.sync
        def _(sp):
            for g in range(CHUNKS):
                sp.dma_start(x_sb[:, chunk(g), :], x_pc[:, chunk(g), :]).then_inc(s_x[g], 16)
            sp.dma_start(w3_sb[:, :, :], w3.rearrange("e (c p) h -> p (e c) h", p=P)).then_inc(s_w3, 16)
            sp.dma_start(w1_sb[:, :, :], w1.rearrange("e h m -> h e m")).then_inc(s_w1, 16)
            sp.dma_start(b1_rows[:, :, :], b1.rearrange("(a e) m -> a e m", a=1).to_broadcast([P, E, M])).then_inc(s_b1, 16)
            sp.dma_start(w2_sb[:, :, :, :].rearrange("p e c m -> p (e c) m"),
                         w2.rearrange("e (c p) m -> p (e c) m", p=P)).then_inc(s_w2, 16)
            sp.dma_start(b2_rows[:, :, :], b2.rearrange("(a e) m -> a e m", a=1).to_broadcast([P, E, M])).then_inc(s_b2, 16)
            for n in range(UNROLL):
                sp.wait_ge(s_scatter[n], 16 * len(range(n, NUM_TILES, UNROLL)))
            y_pc = y_rows[0:TOP_K * TOKENS, :].rearrange("(k p c) h -> p k c h", k=TOP_K, c=COLS)
            for g in range(CHUNKS):
                for k in range(TOP_K):
                    sp.dma_start(y_back[:, k, chunk(g), :], y_pc[:, k, chunk(g), :]).then_inc(s_back[g], 16)
            for g in range(CHUNKS):
                sp.wait_ge(s_out, g + 1)
                sp.dma_start(out_pc[:, chunk(g), :], out_sb[:, chunk(g), :]).then_inc(s_store, 16)
            sp.wait_ge(s_store, 16 * CHUNKS)

        @block.gpsimd
        def _(pool):
            pool.memset(ident[:, :], 0.0).then_inc(s_pool, 1)
            pool.memset(before[:, :], 1.0).then_inc(s_pool, 1)
            pool.memset(ones16[:, :], 1.0)
            pool.memset(ones_row[:, :], 1.0)
            pool.wait_ge(s_pool, 2)
            pool.affine_select(out=ident[:, :], in_=ident[:, :], compare_op=ALU.not_equal, fill=1.0,
                               base=0, pattern=[[-1, P]], channel_multiplier=1).then_inc(s_const, 1)
            pool.affine_select(out=before[:, :], in_=before[:, :], compare_op=ALU.is_ge, fill=0.0,
                               base=-1, pattern=[[1, P]], channel_multiplier=-1)
            pool.iota(lane_i[:, :], pattern=[[1, P]], base=0, channel_multiplier=0)
            pool.iota(rev_e_i[:, :], pattern=[[-1, E]], base=E, channel_multiplier=0)
            pool.iota(thresh_i[:, :], pattern=[[P, COLS]], base=0, channel_multiplier=0)
            pool.iota(token1_i[:, :], pattern=[[1, COLS]], base=1, channel_multiplier=COLS)
            pool.iota(tiles_i[:, :, :], pattern=[[UNROLL, ROWS], [1, ROW]], base=-1, channel_multiplier=0)
            pool.iota(spare_i[:, :], pattern=[[P, TABLE]], base=TOP_K * TOKENS + 1,
                      channel_multiplier=1).then_inc(s_pool, 1)
            pool.memset(zeros_e[:, :], 0.0)
            pool.memset(pick[0][:, :, :], 0.0)
            pool.memset(pick[1][:, :, :], 0.0)
            pool.wait_ge(s_pool, 3)
            pool.tensor_copy(lane16[:, :], lane_i[:, :])
            pool.tensor_copy(rev_e[:, :], rev_e_i[:, :])
            pool.tensor_copy(thresh[:, :], thresh_i[:, :])
            pool.tensor_copy(token1[:, :], token1_i[:, :])
            pool.tensor_copy(tiles_f[:, :, :], tiles_i[:, :, :])
            pool.tensor_copy(spare[:, :], spare_i[:, :])
            pool.wait_ge(s_small, 16 * NUM_SMALL)
            pool.tensor_copy(cond_rep[:, :, :], cond_t[:, :].unsqueeze(2).to_broadcast([G, BATCH, COLS]))
            pool.tensor_tensor(bias_row[:, :], wg_b_sb[:, :], gg_b_sb[:, :], ALU.add).then_inc(s_const, 1)
            pool.wait_ge(s_qhat, 2)
            for i in range(QUAT):
                for k in range(QUAT):
                    a, sign = LEFT[i][k]
                    pool.tensor_scalar(left[:, i, k:k + 1], ql_n[:, a:a + 1], float(sign), None, ALU.mult)
                    a, sign = RIGHT_CONJ[k][i]
                    last = pool.tensor_scalar(right_t[:, i, k:k + 1], qr_n[:, a:a + 1], float(sign), None,
                                              ALU.mult)
            last.then_inc(s_coefs, 1)

            def gather(t, slot_n):
                wait_count(pool, s_t0, t - UNROLL + 1)
                wait_count(pool, s_gidx, t + 1)
                pool.sem_inc(s_go, 1)
                pool.indirect_dma_start(
                    out=x_g[:, slot_n, :], out_offset=None, in_=x_rows,
                    in_offset=bass.IndirectOffsetOnAxis(ap=gather_idx[:, slot_n:slot_n + 1], axis=0),
                ).then_inc(s_gather[slot_n], 16)

            def scatter(t, slot_n):
                wait_count(pool, s_y, t + 1)
                pool.sem_inc(s_go, 1)
                pool.indirect_dma_start(
                    out=y_rows, out_offset=bass.IndirectOffsetOnAxis(
                        ap=scatter_idx[:, slot_n:slot_n + 1], axis=0),
                    in_=y[:, slot_n, :], in_offset=None,
                ).then_inc(s_scatter[slot_n], 16)

            for t in range(5):
                gather(t, t % UNROLL)
            trips = (NUM_TILES - 5) // UNROLL
            with pool.Fori(0, trips) as n:
                for u in range(UNROLL):
                    gather(n * UNROLL + u + 5, (u + 5) % UNROLL)
                    scatter(n * UNROLL + u, u)
            for t in range(5 + trips * UNROLL, NUM_TILES):
                gather(t, t % UNROLL)
            for t in range(trips * UNROLL, NUM_TILES):
                scatter(t, t % UNROLL)

        @block.scalar
        def _(act):
            for dst, src in (
                (rms_sb[:, :], rms_w.rearrange("(h a) -> h a", a=1)),
                (wg_sb[:, :], wg_w),
                (wg_b_sb[:, :], wg_b.rearrange("(a e) -> a e", a=1)),
                (gg_b_sb[:, :], gg_b.rearrange("(a e) -> a e", a=1)),
                (gg_sb[:, :], gg_w),
                (cond_t[:, :], cond.rearrange("b g -> g b")),
                (qr_t[:, :], q_right.rearrange("q d -> d q")),
                (gate_t[:, :], gate.rearrange("a b c d -> d (a b c)")),
                (b3_sb[:, :], b3),
            ):
                act.dma_start(dst, src, allow_slow_non_contiguous=True).then_inc(s_small, 16)
            for g in range(CHUNKS):
                act.wait_ge(s_x[g], 16)
                act.activation(x_sq[:, chunk(g), :], x_sb[:, chunk(g), :], ACT.Square).then_inc(s_sq, 1)
                act.wait_ge(s_tr, g + 1)
                act.activation(x_t[:, chunk(g), :], bank[g % 2][:, :], ACT.Copy).then_inc(s_xt, 1)
            act.wait_ge(s_qn, 1)
            act.activation(q_root[:, :], q_norm[:, :], ACT.Sqrt).then_inc(s_qroot, 1)
            act.wait_ge(s_var, 1)
            act.activation(rms[:, :], var[:, :], ACT.Sqrt).then_inc(s_rms, 1)
            act.wait_ge(s_shift, 1)
            act.activation(expv[:, :, :], logits[:, :, :], ACT.Exp).then_inc(s_exp, 1)
            for g in range(CHUNKS):
                act.wait_ge(s_w3tp, g + 1)
                act.activation(w3_t[:, chunk(g), :], bank[6 + g % 2][:, :], ACT.Copy).then_inc(s_w3t, 1)
            act.wait_ge(s_b3tp, 1)
            act.activation(b3_t[:, :], bank[1][:, 0:E], ACT.Copy).then_inc(s_b3t, 1)
            act.wait_ge(s_b3t, 1)
            act.activation(b3_cols[:, :, :], b3_t[:, :].unsqueeze(2).to_broadcast([H, E, P]),
                           ACT.Copy).then_inc(s_b3t, 1)
            for g in range(CHUNKS):
                act.wait_ge(s_w3rp, g + 1)
                act.activation(w3_rot[:, chunk(g), :], bank[6 + g % 2][:, :], ACT.Copy).then_inc(s_w3r, 1)
            for g in range(2):
                act.wait_ge(s_b3rp, g + 1)
                act.activation(b3_rows[:, 4 * g:4 * g + 4, :], bank[6 + g % 2][:, :], ACT.Copy).then_inc(s_b3r, 1)
            for g in range(CHUNKS):
                act.wait_ge(s_xrp, g + 1)
                act.activation(base[:, chunk(g), :], bank[6 + g % 2][:, :], ACT.Copy).then_inc(s_base, 1)

            def copy_tile_t(t):
                act.wait_ge(s_t0, t + 1)
                wait_count(act, s_l1, t)
                act.activation(x_gt[:, :], bank[0][:, 0:P], ACT.Copy).then_inc(s_xgt, 1)

            def relu1(t):
                act.wait_ge(s_t1, t + 1)
                wait_count(act, s_l2, t)
                act.activation(h1_t[:, :, :], bank[2][:, 0:M], ACT.Relu).then_inc(s_h1t, 1)

            def relu2(t):
                act.wait_ge(s_t2, t + 1)
                wait_count(act, s_l3, t)
                act.activation(h2_t[:, :, :], bank[4][:, 0:M], ACT.Relu).then_inc(s_h2t, 1)

            def peeled(i):
                if 0 <= i + 1 < NUM_TILES:
                    relu1(i + 1)
                if i + 2 < NUM_TILES:
                    copy_tile_t(i + 2)
                if 0 <= i < NUM_TILES:
                    relu2(i)

            for i in range(-2, FIRST_STEADY):
                peeled(i)
            with act.Fori(0, STEADY_TRIPS) as n:
                for u in range(UNROLL):
                    i = n * UNROLL + (FIRST_STEADY + u)
                    relu1(i + 1)
                    copy_tile_t(i + 2)
                    relu2(i)
            for i in range(PEEL_AFTER, LAST_STEP + 1):
                peeled(i)

        @block.vector
        def _(dve):
            steps = [0]

            def step(instruction):
                steps[0] += 1
                instruction.then_inc(s_dve, 1)
                dve.wait_ge(s_dve, steps[0])

            def over_e(ap):
                return ap.unsqueeze(2).to_broadcast([P, COLS, E])

            dve.wait_ge(s_small, 16 * NUM_SMALL)
            dve.wait_ge(s_const, 2)
            dve.tensor_scalar(wg_rms[:, :], wg_sb[:, :], rms_sb[:, :], None, ALU.mult).then_inc(s_wgr, 1)
            dve.tensor_tensor(q_sq[:, 0:BATCH], cond_t[:, :], cond_t[:, :], ALU.mult)
            step(dve.tensor_tensor(q_sq[:, BATCH:], qr_t[:, :], qr_t[:, :], ALU.mult))
            dve.tensor_reduce(q_norm[:, 0:1], q_sq[:, 0:BATCH], X_AXIS, ALU.add)
            step(dve.tensor_reduce(q_norm[:, 1:2], q_sq[:, BATCH:], X_AXIS, ALU.add))
            dve.tensor_scalar(q_norm[:, :], q_norm[:, :], EPS_QUAT, None, ALU.add).then_inc(s_qn, 1)

            for g in range(CHUNKS):
                dve.wait_ge(s_sq, g + 1)
                last = dve.tensor_reduce(var[:, chunk(g)], x_sq[:, chunk(g), :], X_AXIS, ALU.add)
            step(last)
            dve.tensor_scalar(var[:, :], var[:, :], 1.0 / H, EPS_RMS, ALU.mult, ALU.add).then_inc(s_var, 1)
            dve.wait_ge(s_qroot, 1)
            step(dve.reciprocal(q_inv[:, :], q_root[:, :]))
            dve.tensor_scalar(ql_n[:, :], cond_t[:, 0:QUAT], q_inv[:, 0:1], None, ALU.mult).then_inc(s_qhat, 1)
            dve.tensor_scalar(qr_n[:, :], qr_t[:, :], q_inv[:, 1:2], gate_t[:, :], ALU.mult, ALU.mult).then_inc(s_qhat, 1)
            dve.wait_ge(s_rms, 1)
            step(dve.reciprocal(rstd[:, :], rms[:, :]))

            dve.wait_ge(s_logit, 1)
            step(dve.tensor_tensor(logits[:, :, :], bank[2][:, 0:P].rearrange("p (c e) -> p c e", e=E),
                                   over_e(rstd[:, :]), ALU.mult))
            dve.wait_ge(s_bias, 1)
            step(dve.tensor_tensor(logits[:, :, :], logits[:, :, :],
                                   bank[3][:, 0:E].unsqueeze(1).to_broadcast([P, COLS, E]), ALU.add))
            step(dve.tensor_reduce(row_max[:, :], logits[:, :, :], X_AXIS, ALU.max))
            dve.tensor_tensor(logits[:, :, :], logits[:, :, :], over_e(row_max[:, :]),
                              ALU.subtract).then_inc(s_shift, 1)
            dve.wait_ge(s_coefs, 1)
            step(dve.tensor_tensor(lr_prod[:, :, :, :], left[:, :, :].unsqueeze(1).to_broadcast([QD, QUAT, QUAT, QUAT]),
                                   right_t[:, :, :].unsqueeze(2).to_broadcast([QD, QUAT, QUAT, QUAT]), ALU.mult))
            step(dve.tensor_reduce(coef[:, :, :], lr_prod[:, :, :, :], X_AXIS, ALU.add))
            for j in range(QUAT):
                last = dve.tensor_tensor(rot0[QD * j:QD * (j + 1), :].rearrange("p (i d) -> p i d", i=QUAT),
                                         ident[0:QD, 0:QD].unsqueeze(1).to_broadcast([QD, QUAT, QD]),
                                         coef[:, j, :].unsqueeze(2).to_broadcast([QD, QUAT, QD]), ALU.mult)
            step(last)
            dve.tensor_tensor(rot[:, :], rot0[:, :], ident[:, :], ALU.add).then_inc(s_rot, 1)
            dve.wait_ge(s_exp, 1)
            step(dve.tensor_reduce(row_sum[:, :], expv[:, :, :], X_AXIS, ALU.add))
            step(dve.reciprocal(row_sum[:, :], row_sum[:, :]))
            step(dve.tensor_tensor(probs[:, :, :], expv[:, :, :], over_e(row_sum[:, :]), ALU.mult))
            dve.wait_ge(s_const, 2)
            rev = rev_e[:, :].unsqueeze(1).to_broadcast([P, COLS, E])
            for k in range(TOP_K):
                step(dve.tensor_reduce(weight[:, k, :], probs[:, :, :], X_AXIS, ALU.max))
                step(dve.tensor_tensor(key[:, :, :], probs[:, :, :], over_e(weight[:, k, :]), ALU.is_equal))
                step(dve.tensor_tensor(key[:, :, :], key[:, :, :], rev, ALU.mult))
                step(dve.tensor_reduce(key_max[:, :], key[:, :, :], X_AXIS, ALU.max))
                step(dve.tensor_tensor(chosen[:, k, :, :], rev, over_e(key_max[:, :]), ALU.is_equal))
                if k == 0:
                    step(dve.scalar_tensor_tensor(out=probs[:, :, :], in0=chosen[:, 0, :, :], scalar=-2.0,
                                                  in1=probs[:, :, :], op0=ALU.mult, op1=ALU.add))
            dve.tensor_tensor(pick_one[:, :, :], chosen[:, 0, :, :], chosen[:, 1, :, :], ALU.add)
            step(dve.tensor_tensor(pick[0][:, COLS:, :], chosen[:, 0, :, :], chosen[:, 1, :, :], ALU.add))
            src, dst = 0, 1
            for shift in (1, 2, 4, 8):
                ins = dve.tensor_tensor(pick[dst][:, COLS:, :], pick[src][:, COLS:, :],
                                        pick[src][:, COLS - shift:2 * COLS - shift, :], ALU.add)
                if shift == 8:
                    ins.then_inc(s_pick, 1)
                else:
                    step(ins)
                src, dst = dst, src
            dve.wait_ge(s_rank, 1)
            step(dve.tensor_tensor(over[:, :, :], bank[4][:, 0:E].unsqueeze(2).to_broadcast([P, E, COLS]),
                                   thresh[:, :].unsqueeze(1).to_broadcast([P, E, COLS]), ALU.is_gt))
            step(dve.tensor_reduce(tile_count[:, :], over[:, :, :], X_AXIS, ALU.add))
            step(dve.tensor_tensor_scan(tile_end[:, :], tile_count[:, :], zeros_e[:, :], 0.0, ALU.add, ALU.add))
            step(dve.tensor_tensor(tile_start[:, :], tile_end[:, :], tile_count[:, :], ALU.subtract))
            step(dve.scalar_tensor_tensor(
                out=position[:, :, :], in0=tile_start[:, :].unsqueeze(1).to_broadcast([P, COLS, E]),
                scalar=float(P), in1=bank[5][:, 0:P].rearrange("p (c e) -> p c e", e=E),
                op0=ALU.mult, op1=ALU.add))
            step(dve.tensor_tensor(pos_chosen[:, :, :, :].rearrange("p k c e -> p k (c e)"),
                                   chosen[:, :, :, :].rearrange("p k c e -> p k (c e)"),
                                   position[:, :, :].rearrange("p c e -> p (c e)").unsqueeze(1).to_broadcast(
                                       [P, TOP_K, COLS * E]), ALU.mult))
            step(dve.tensor_reduce(slot[:, :], pos_chosen[:, :, :, :].rearrange("p k c e -> p (k c) e"),
                                   X_AXIS, ALU.add))
            step(dve.tensor_copy(slot_i[:, :], slot[:, :]))
            dve.tensor_scalar(tile_of_i[:, :], slot_i[:, :], 7, None, ALU.arith_shift_right)
            step(dve.tensor_scalar(lane_of_i[:, :], slot_i[:, :], P - 1, None, ALU.bitwise_and))
            dve.tensor_copy(tile_of[:, :], tile_of_i[:, :])
            step(dve.tensor_copy(lane_of[:, :], lane_of_i[:, :]))
            for n in range(PAIRS):
                c = n % COLS
                dve.tensor_scalar(tile_hot[:, n, :], lane16[:, 0:TABLE], tile_of[:, n:n + 1],
                                  token1[:, c:c + 1], ALU.is_equal, ALU.mult)
                dve.tensor_scalar(lane_hot[:, n, :], lane16[:, :], lane_of[:, n:n + 1], None,
                                  ALU.is_equal).then_inc(s_hot, 1)
            dve.tensor_tensor(ended[:, :, :], tiles_f[:, :, :].rearrange("a r k -> a (r k)").unsqueeze(2).to_broadcast([1, ROWS * ROW, E]),
                              tile_end[0:1, :].unsqueeze(1).to_broadcast([1, ROWS * ROW, E]), ALU.is_ge).then_inc(s_dve, 1)
            steps[0] += 1
            dve.wait_ge(s_dve, steps[0])
            step(dve.tensor_reduce(expert_f[:, :], ended[:, :, :], X_AXIS, ALU.add))
            dve.tensor_scalar(tile_expert[:, :, :].rearrange("a r k -> a (r k)"), expert_f[:, :], float(E - 1), None, ALU.min).then_inc(s_tables, 1)
            dve.wait_ge(s_inv, 1)
            step(dve.tensor_copy(second[:, :], bank[3][:, 0:TABLE]))
            step(dve.tensor_tensor(filled[:, :], bank[2][:, 0:TABLE], second[:, :], ALU.add))
            step(dve.tensor_scalar(gather_f[:, :], filled[:, :], -1.0, 0.0, ALU.add, ALU.max))
            dve.tensor_copy(gather_row[:, :], gather_f[:, :]).then_inc(s_tables, 1)
            dve.tensor_scalar(is_second[:, :], second[:, :], 0.0, float(TOKENS), ALU.is_gt, ALU.mult)
            step(dve.scalar_tensor_tensor(out=is_unused[:, :], in0=filled[:, :], scalar=0.0, in1=spare[:, :],
                                          op0=ALU.is_equal, op1=ALU.mult))
            step(dve.tensor_tensor(row_1[:, :], filled[:, :], is_second[:, :], ALU.add))
            step(dve.scalar_tensor_tensor(out=row_1[:, :], in0=row_1[:, :], scalar=-1.0, in1=is_unused[:, :],
                                          op0=ALU.add, op1=ALU.add))
            step(dve.tensor_copy(scatter_row[:, :], row_1[:, :]))


            def set_gather(t, slot_n):
                wait_count(dve, s_t0, t - UNROLL + 1)
                dve.tensor_copy(gather_idx[:, slot_n:slot_n + 1],
                                gather_row[:, bass.ds(t, 1)]).then_inc(s_gidx, 1)

            def bias1(t, e):
                dve.wait_ge(s_l1, t + 1)
                wait_count(dve, s_t1, t)
                dve.tensor_tensor(h1[:, :], bank[1][:, 0:M], expert_rows(b1_rows, e), ALU.add).then_inc(s_h1, 1)

            def bias2(t, e):
                dve.wait_ge(s_l2, t + 1)
                wait_count(dve, s_t2, t)
                dve.tensor_tensor(h2[:, :], bank[3][:, 0:M], expert_rows(b2_rows, e), ALU.add).then_inc(s_h2, 1)

            def bias3(t, e, slot_n, round_n):
                dve.wait_ge(s_l3, t + 1)
                wait_count(dve, s_scatter[slot_n], 16 * round_n)
                dve.tensor_copy(scatter_idx[:, slot_n:slot_n + 1],
                                scatter_row[:, bass.ds(t, 1)])
                dve.tensor_tensor(y[:, slot_n, :], bank[5][:, 0:H], expert_rows(b3_rows, e), ALU.add).then_inc(s_y, 1)


            def peeled(i, experts):
                if 0 <= i + 1 < NUM_TILES:
                    bias1(i + 1, experts[i + 1])
                if 0 <= i < NUM_TILES:
                    bias2(i, experts[i])
                if 0 <= i - 1 < NUM_TILES:
                    bias3(i - 1, experts[i - 1], (i - 1) % UNROLL, (i - 1) // UNROLL)
                if i + 5 < TABLE:
                    set_gather(i + 5, (i + 5) % UNROLL)

            dve.wait_ge(s_dve, steps[0])
            dve.wait_ge(s_tables, 2)
            for t in range(UNROLL):
                set_gather(t, t)
            dve.wait_ge(s_b1, 16)
            dve.wait_ge(s_b2, 16)
            dve.wait_ge(s_b3r, 2)
            early, live, ahead = expert_registers(dve)
            dve.reg_load(early, tile_expert[0:1, 0:EARLY_ROWS, :].rearrange("a r k -> a (r k)"))
            experts = {UNROLL * (k // ROW) - 1 + k % ROW: as_expert(dve, early[k]) for k in range(1, len(early))}
            for i in range(-2, FIRST_STEADY):
                peeled(i, experts)
            for k in range(LIVE):
                dve.reg_mov(live[k], experts[FIRST_STEADY - 1 + k])
            with dve.Fori(0, STEADY_TRIPS) as n:
                first = n * UNROLL + FIRST_STEADY
                experts = [as_expert(dve, r) for r in live]
                for u in range(UNROLL):
                    i = first + u
                    bias1(i + 1, experts[u + 2])
                    bias2(i, experts[u + 1])
                    bias3(i - 1, experts[u], u, n + (FIRST_STEADY - 1) // UNROLL)
                    set_gather(i + 5, u)
                    if u == 1:
                        load_ahead(dve, ahead, tile_expert, n)
                next_trip(dve, live, ahead)
            experts = {PEEL_AFTER - 1 + k: as_expert(dve, live[k]) for k in range(3)}
            for i in range(PEEL_AFTER, LAST_STEP + 1):
                peeled(i, experts)

            dve.wait_ge(s_base, CHUNKS)
            for g in range(CHUNKS):
                dve.wait_ge(s_back[g], 16 * TOP_K)
                for c in range(g * CPC, (g + 1) * CPC):
                    last = dve.scalar_tensor_tensor(out=partial[:, c, :], in0=y_back[:, 0, c, :],
                                                    scalar=weight[:, 0, c:c + 1], in1=base[:, c, :],
                                                    op0=ALU.mult, op1=ALU.add)
                last.then_inc(s_partial, 1)
                dve.wait_ge(s_partial, g + 1)
                for c in range(g * CPC, (g + 1) * CPC):
                    last = dve.scalar_tensor_tensor(out=out_sb[:, c, :], in0=y_back[:, 1, c, :],
                                                    scalar=weight[:, 1, c:c + 1], in1=partial[:, c, :],
                                                    op0=ALU.mult, op1=ALU.add)
                last.then_inc(s_out, 1)

        @block.tensor
        def _(pe):
            def transpose_x(g):
                pe.wait_ge(s_x[g], 16)
                wait_count(pe, s_xt, g - 1)
                for j in range(CPC):
                    last = pe.transpose(bank[g % 2][:, j * P:(j + 1) * P], x_sb[:, g * CPC + j, :], ident[:, :])
                last.then_inc(s_tr, 1)

            def gate_logits(g):
                pe.wait_ge(s_xt, g + 1)
                for c in range(g * CPC, (g + 1) * CPC):
                    last = pe.matmul(bank[2][:, c * E:(c + 1) * E], x_t[:, c, :], wg_rms[:, :],
                                     start=True, stop=True)
                return last

            pe.wait_ge(s_const, 1)
            transpose_x(0)
            transpose_x(1)
            pe.wait_ge(s_wgr, 1)
            gate_logits(0)
            transpose_x(2)
            gate_logits(1)
            transpose_x(3)
            gate_logits(2)
            gate_logits(3).then_inc(s_logit, 1)
            pe.wait_ge(s_small, 16 * NUM_SMALL)
            pe.wait_ge(s_const, 2)
            pe.matmul(bank[3][:, 0:E], cond_rep[:, :, :].rearrange("g b c -> g (b c)"), gg_sb[:, :],
                      start=True, stop=False)
            pe.matmul(bank[3][:, 0:E], ones_row[:, :], bias_row[:, :], start=False, stop=True).then_inc(s_bias, 1)
            pe.wait_ge(s_w3, 16)
            for g in range(CHUNKS):
                wait_count(pe, s_w3t, g - 1)
                for j in range(CPC):
                    last = pe.transpose(bank[6 + g % 2][:, j * P:(j + 1) * P], w3_sb[:, g * CPC + j, :], ident[:, :])
                last.then_inc(s_w3tp, 1)
            pe.transpose(bank[1][:, 0:E], b3_sb[:, :], ident[0:E, 0:E]).then_inc(s_b3tp, 1)
            pe.wait_ge(s_pick, 1)
            pe.matmul(bank[5][:, 0:P], before[:, :], pick_one[:, :, :].rearrange("p c e -> p (c e)"),
                      start=True, stop=False)
            pe.matmul(bank[5][:, 0:P], ones16[:, :],
                      pick[0][:, COLS - 1:2 * COLS - 1, :].rearrange("p c e -> p (c e)"), start=False, stop=True)
            pe.matmul(bank[4][:, 0:E], ones16[:, :], pick[0][:, 2 * COLS - 1, :],
                      start=True, stop=True).then_inc(s_rank, 1)
            pe.wait_ge(s_rot, 1)
            for g in range(CHUNKS):
                pe.wait_ge(s_w3t, CHUNKS)
                wait_count(pe, s_w3r, g - 1)
                for j in range(CPC):
                    last = pe.matmul(bank[6 + g % 2][:, j * P:(j + 1) * P], w3_t[:, g * CPC + j, :], rot[:, :],
                                     start=True, stop=True)
                last.then_inc(s_w3rp, 1)
            pe.wait_ge(s_b3t, 2)
            for g in range(2):
                pe.wait_ge(s_w3r, 3 + g)
                for j in range(4):
                    last = pe.matmul(bank[6 + g][:, j * H:(j + 1) * H], b3_cols[:, 4 * g + j, :], rot[:, :],
                                     start=True, stop=True)
                last.then_inc(s_b3rp, 1)
            for n in range(PAIRS):
                pe.wait_ge(s_hot, n + 1)
                last = pe.matmul(bank[2 + n // COLS][:, 0:TABLE], lane_hot[:, n, :], tile_hot[:, n, :],
                                 start=n % COLS == 0, stop=n % COLS == COLS - 1)
            last.then_inc(s_inv, 1)
            for g in range(CHUNKS):
                pe.wait_ge(s_b3r, min(g + 1, 2))
                wait_count(pe, s_base, g - 1)
                for j in range(CPC):
                    last = pe.matmul(bank[6 + g % 2][:, j * H:(j + 1) * H], x_t[:, g * CPC + j, :], rot[:, :],
                                     start=True, stop=True)
                last.then_inc(s_xrp, 1)

            def transpose_tile(t, slot_n, round_n):
                pe.wait_ge(s_gather[slot_n], 16 * (round_n + 1))
                wait_count(pe, s_xgt, t)
                pe.transpose(bank[0][:, 0:P], x_g[:, slot_n, :], ident[:, :]).then_inc(s_t0, 1)

            def layer1(t, e):
                pe.wait_ge(s_xgt, t + 1)
                wait_count(pe, s_h1, t)
                pe.matmul(bank[1][:, 0:M], x_gt[:, :], expert_rows(w1_sb, e), start=True, stop=True).then_inc(s_l1, 1)

            def transpose_h1(t):
                pe.wait_ge(s_h1, t + 1)
                wait_count(pe, s_h1t, t)
                for c in range(MC):
                    last = pe.transpose(bank[2][:, c * P:(c + 1) * P], h1[:, c * P:(c + 1) * P], ident[:, :])
                last.then_inc(s_t1, 1)

            def layer2(t, e):
                pe.wait_ge(s_h1t, t + 1)
                wait_count(pe, s_h2, t)
                for c in range(MC):
                    last = pe.matmul(bank[3][:, 0:M], h1_t[:, c, :],
                                     w2_sb[:, bass.ds(e, 1), c, :].rearrange("p a m -> p (a m)"),
                                     start=c == 0, stop=c == MC - 1)
                last.then_inc(s_l2, 1)

            def transpose_h2(t):
                pe.wait_ge(s_h2, t + 1)
                wait_count(pe, s_h2t, t)
                for c in range(MC):
                    last = pe.transpose(bank[4][:, c * P:(c + 1) * P], h2[:, c * P:(c + 1) * P], ident[:, :])
                last.then_inc(s_t2, 1)

            def layer3(t, e):
                pe.wait_ge(s_h2t, t + 1)
                wait_count(pe, s_y, t)
                for c in range(MC):
                    last = pe.matmul(bank[5][:, 0:H], h2_t[:, c, :],
                                     w3_by_e[:, bass.ds(e, 1), c, :].rearrange("p a m -> p (a m)"),
                                     start=c == 0, stop=c == MC - 1)
                last.then_inc(s_l3, 1)


            def peeled(i, experts):
                if 0 <= i + 1 < NUM_TILES:
                    layer1(i + 1, experts[i + 1])
                if 0 <= i < NUM_TILES:
                    layer2(i, experts[i])
                if 0 <= i + 1 < NUM_TILES:
                    transpose_h1(i + 1)
                if i + 2 < NUM_TILES:
                    transpose_tile(i + 2, (i + 2) % UNROLL, (i + 2) // UNROLL)
                if 0 <= i - 1 < NUM_TILES:
                    layer3(i - 1, experts[i - 1])
                if 0 <= i < NUM_TILES:
                    transpose_h2(i)

            w3_by_e = w3_rot[:, :, :].rearrange("p (e c) h -> p e c h", c=MC)
            pe.wait_ge(s_tables, 1)
            pe.wait_ge(s_w1, 16)
            pe.wait_ge(s_w2, 16)
            pe.wait_ge(s_w3r, CHUNKS)
            early, live, ahead = expert_registers(pe)
            pe.reg_load(early, tile_expert[0:1, 0:EARLY_ROWS, :].rearrange("a r k -> a (r k)"))
            experts = {UNROLL * (k // ROW) - 1 + k % ROW: as_expert(pe, early[k]) for k in range(1, len(early))}
            for i in range(-2, FIRST_STEADY):
                peeled(i, experts)
            for k in range(LIVE):
                pe.reg_mov(live[k], experts[FIRST_STEADY - 1 + k])
            with pe.Fori(0, STEADY_TRIPS) as n:
                first = n * UNROLL + FIRST_STEADY
                experts = [as_expert(pe, r) for r in live]
                for u in range(UNROLL):
                    i = first + u
                    layer1(i + 1, experts[u + 2])
                    layer2(i, experts[u + 1])
                    if u == 1:
                        load_ahead(pe, ahead, tile_expert, n)
                    transpose_h1(i + 1)
                    transpose_tile(i + 2, u, n + (FIRST_STEADY + 2) // UNROLL)
                    layer3(i - 1, experts[u])
                    transpose_h2(i)
                next_trip(pe, live, ahead)
            experts = {PEEL_AFTER - 1 + k: as_expert(pe, live[k]) for k in range(3)}
            for i in range(PEEL_AFTER, LAST_STEP + 1):
                peeled(i, experts)


def expert_registers(engine):
    return [[engine.alloc_register(f"{name}{k}") for k in range(count)]
            for name, count in (("early", EARLY_ROWS * ROW), ("live", LIVE), ("ahead", ROW))]


def as_expert(engine, register):
    return engine.snap(register, min_val=0, max_val=E - 1)


def load_ahead(engine, ahead, tile_expert, n):
    row = n + ((FIRST_STEADY + 2) // UNROLL + 1)
    engine.reg_load(ahead, tile_expert[0:1, bass.ds(row, 1), :].rearrange("a r k -> a (r k)"))


def next_trip(engine, live, ahead):
    engine.reg_mov(live[0], live[UNROLL])
    engine.reg_mov(live[1], live[UNROLL + 1])
    for k in range(UNROLL):
        engine.reg_mov(live[2 + k], ahead[k])


def expert_rows(table, e):
    return table[:, bass.ds(e, 1), :].rearrange("p a m -> p (a m)")


INPUTS = ["x", "cond_256", "L0_cond_rms_w", "L0_cond_wg_W", "L0_cond_wg_b", "L0_cond_gg_W", "L0_cond_gg_b",
          "L0_cond_W1", "L0_cond_b1", "L0_cond_W2", "L0_cond_b2", "L0_cond_W3", "L0_cond_b3",
          "L1_cond_q_right", "L1_cond_spectral_gate"]


def kernel(**inputs):
    import numpy as np
    import concourse.bacc as bacc
    from concourse.bass_utils import run_bass_kernel_spmd

    nc = bacc.Bacc("TRN2", target_bir_lowering=False, num_devices=1)
    arrays, args = {}, []
    for name in INPUTS:
        a = np.ascontiguousarray(inputs[name])
        arrays[f"in_{name}"] = a
        args.append(nc.dram_tensor(f"in_{name}", a.shape, mybir.dt.from_np(a.dtype), kind="ExternalInput").ap())
    out = nc.dram_tensor("out_rotated", (BATCH, SEQ, H), F32, kind="ExternalOutput").ap()
    moe_rotation(nc, *args, out)
    result = run_bass_kernel_spmd(nc, [arrays], core_ids=[0])
    return result.results[0]["out_rotated"]
```

```python
from contextlib import ExitStack

import concourse.bass as bass
from concourse import mybir

F32 = mybir.dt.float32
F16 = mybir.dt.float16
I32 = mybir.dt.int32
ALU = mybir.AluOpType
ACT = mybir.ActivationFunctionType
X_AXIS = mybir.AxisListType.X

P = 128
BATCH, SEQ, H = 8, 256, 128
TOKENS = BATCH * SEQ
COLS = TOKENS // P
E, M, G = 8, 256, 32
TOP_K = 2
PAIRS = TOP_K * COLS
MC = M // P
UNROLL = 3
NUM_TILES = (TOP_K * TOKENS + E * (P - 1)) // P
TABLE = NUM_TILES + 1
QUAT = 4
QD = H // QUAT
CHUNKS = 4
CPC = COLS // CHUNKS
X_LOADS = 2
MASK = -3.0e38
HOT_PARTS = 8
GATHERS_AHEAD = 5
EPS_RMS = 1e-6
EPS_QUAT = 1e-8

LEFT = [[(0, 1), (1, -1), (2, -1), (3, -1)],
        [(1, 1), (0, 1), (3, -1), (2, 1)],
        [(2, 1), (3, 1), (0, 1), (1, -1)],
        [(3, 1), (2, -1), (1, 1), (0, 1)]]
RIGHT_CONJ = [[(0, 1), (1, 1), (2, 1), (3, 1)],
              [(1, -1), (0, 1), (3, -1), (2, 1)],
              [(2, -1), (3, 1), (0, 1), (1, -1)],
              [(3, -1), (2, -1), (1, 1), (0, 1)]]

FIRST_STEADY = 4
LAST_STEP = NUM_TILES
STEADY_TRIPS = (NUM_TILES - 2 - FIRST_STEADY) // UNROLL
PEEL_AFTER = FIRST_STEADY + STEADY_TRIPS * UNROLL

ROW = 4
LIVE = UNROLL + 2
EARLY_ROWS = 3
ROWS = (FIRST_STEADY + 2) // UNROLL + STEADY_TRIPS + 1


def wait_count(engine, semaphore, count):
    if isinstance(count, int) and count <= 0:
        return
    engine.wait_ge(semaphore, count)


def moe_rotation(nc, x, cond, rms_w, wg_w, wg_b, gg_w, gg_b, w1, b1, w2, b2, w3, b3,
                 q_right, gate, out):
    y_rows = nc.dram_tensor("y_rows", (TOP_K * TOKENS + TABLE * P, H), F32, kind="Internal").ap()

    with ExitStack() as ctx:
        def sb(name, shape, dt=F32):
            return ctx.enter_context(nc.sbuf_tensor(name, shape, dt))

        def ps(name, shape):
            return ctx.enter_context(nc.psum_tensor(name, shape, F32))

        def sem(name):
            return ctx.enter_context(nc.semaphore(name))

        x_sb = sb("x_sb", [P, COLS, H])
        w1_sb = sb("w1_sb", [P, E * M])
        w2_sb = sb("w2_sb", [P, MC * E * M])
        w3_sb = sb("w3_sb", [P, E * MC, H])
        b1_rows = sb("b1_rows", [P, E * M])
        b2_rows = sb("b2_rows", [P, E * M])
        b3_sb = sb("b3_sb", [E, H])
        rms_sb = sb("rms_sb", [H, 1])
        wg_sb = sb("wg_sb", [H, E])
        gate_b_sb = sb("gate_b_sb", [1, 2, E])
        gg_sb = sb("gg_sb", [G, E])
        cond_t = sb("cond_t", [G, BATCH])
        qr_t = sb("qr_t", [QD, QUAT])
        gate_t = sb("gate_t", [QD, 1])

        ident = sb("ident", [P, P])
        before = sb("before", [P, P], F16)
        ones16 = sb("ones16", [P, P], F16)
        ones_row = sb("ones_row", [1, P])
        lane_i = sb("lane_i", [P, P], I32)
        lane16 = sb("lane16", [P, P], F16)
        rev_e_i = sb("rev_e_i", [P, E], I32)
        rev_e = sb("rev_e", [P, E])
        minus16 = sb("minus16", [P, P], F16)
        thresh_i = sb("thresh_i", [P, COLS], I32)
        thresh = sb("thresh", [P, COLS])
        token1_i = sb("token1_i", [P, COLS], I32)
        token1 = sb("token1", [P, COLS])
        spare_i = sb("spare_i", [P, TABLE], I32)
        spare = sb("spare", [P, TABLE])
        tiles_i = sb("tiles_i", [1, ROWS, ROW], I32)
        tiles_f = sb("tiles_f", [1, ROWS, ROW])
        zeros_e = sb("zeros_e", [P, E])

        x_sq = sb("x_sq", [P, COLS, H])
        x_t = sb("x_t", [H, COLS, P])
        wg_rms = sb("wg_rms", [H, E])
        cond_rep = sb("cond_rep", [G, BATCH, COLS])
        var = sb("var", [P, COLS])
        rms = sb("rms", [P, COLS])
        rstd = sb("rstd", [P, COLS])
        logits = sb("logits", [P, COLS, E])
        best = sb("best", [P, TOP_K, COLS])
        rest = sb("rest", [P, COLS, E])
        shifted = sb("shifted", [P, COLS, E])
        shifted_best = sb("shifted_best", [P, TOP_K, COLS])
        exp_best = sb("exp_best", [P, TOP_K, COLS])
        expv = sb("expv", [P, COLS, E])
        row_sum = sb("row_sum", [P, COLS])
        weight = sb("weight", [P, TOP_K, COLS])
        key = sb("key", [P, COLS, E])
        key_max = sb("key_max", [P, COLS])
        chosen = sb("chosen", [P, TOP_K, COLS, E])
        picks = sb("picks", [P, E, COLS], F16)
        picks_before = sb("picks_before", [P, E * COLS + 1], F16)
        zeros16 = sb("zeros16", [P, E * COLS], F16)
        over = sb("over", [P, E, COLS])
        tile_count = sb("tile_count", [P, E])
        tile_end = sb("tile_end", [P, E])
        tile_start = sb("tile_start", [P, E])
        position = sb("position", [P, E, COLS])
        pos_chosen = sb("pos_chosen", [P, TOP_K, COLS, E])
        slot_i = sb("slot_i", [P, PAIRS], I32)
        lane_of_i = sb("lane_of_i", [P, PAIRS], I32)
        tile_of_i = sb("tile_of_i", [P, PAIRS], I32)
        lane_hot = sb("lane_hot", [P, PAIRS, P], F16)
        tile_is = sb("tile_is", [P, PAIRS, TABLE], F16)
        tile_hot = sb("tile_hot", [P, PAIRS, TABLE], F16)
        second = sb("second", [P, TABLE])
        filled = sb("filled", [P, TABLE])
        is_second = sb("is_second", [P, TABLE])
        is_unused = sb("is_unused", [P, TABLE])
        row_1 = sb("row_1", [P, TABLE])
        gather_f = sb("gather_f", [P, TABLE])
        gather_row = sb("gather_row", [P, TABLE], I32)
        scatter_row = sb("scatter_row", [P, TABLE], I32)
        ended = sb("ended", [1, ROWS * ROW, E])
        expert_f = sb("expert_f", [1, ROWS * ROW])
        tile_row = sb("tile_row", [1, ROWS, ROW], I32)

        q_sq = sb("q_sq", [QD, BATCH + QUAT])
        q_norm = sb("q_norm", [QD, 2])
        q_root = sb("q_root", [QD, 2])
        q_inv = sb("q_inv", [QD, 2])
        ql_n = sb("ql_n", [QD, QUAT])
        qr_n = sb("qr_n", [QD, QUAT])
        left = sb("left", [QD, QUAT, QUAT])
        right_t = sb("right_t", [QD, QUAT, QUAT])
        lr_prod = sb("lr_prod", [QD, QUAT, QUAT, QUAT])
        coef = sb("coef", [QD, QUAT, QUAT])
        rot0 = sb("rot0", [H, H])
        rot = sb("rot", [H, H])
        w3_t = sb("w3_t", [H, E * MC, P])
        w3_rot = sb("w3_rot", [P, E * M])
        b3_t = sb("b3_t", [H, E])
        b3_cols = sb("b3_cols", [H, E, P])
        b3_rows = sb("b3_rows", [P, E, 2, H])
        base = sb("base", [P, COLS, H])

        x_g = sb("x_g", [P, UNROLL, H])
        x_gt = sb("x_gt", [H, P])
        h1 = sb("h1", [P, M])
        h1_t = sb("h1_t", [P, MC, P])
        h2 = sb("h2", [P, M])
        h2_t = sb("h2_t", [P, MC, P])
        y = sb("y", [P, UNROLL, H])
        y_back = sb("y_back", [P, TOP_K, COLS, H])
        partial = sb("partial", [P, COLS, H])
        scaled = sb("scaled", [P, COLS, H])
        out_sb = sb("out_sb", [P, COLS, H])

        bank = [ps(f"bank{n}", [P, 512]) for n in range(8)]

        s_x = [sem(f"x_loaded{g}") for g in range(X_LOADS)]
        s_router_in, s_quat_in = sem("router_weights_loaded"), sem("quaternions_loaded")
        s_bias_in, s_b3_in = sem("gate_biases_loaded"), sem("b3_loaded")
        s_w1, s_w2, s_w3 = sem("w1_loaded"), sem("w2_loaded"), sem("w3_loaded")
        s_b1, s_b2 = sem("b1_loaded"), sem("b2_loaded")
        s_const = sem("constants_made")
        s_pool = sem("pool_steps")
        s_coefs = sem("quaternion_signs_placed")
        s_sq = sem("x_squared")
        s_tr = sem("x_transposed")
        s_xt = sem("x_t_copied")
        s_wgr = sem("wg_rms_made")
        s_bias = sem("gate_bias_done")
        s_logit = sem("logits_done")
        s_var, s_rms, s_qn, s_qroot = sem("var_made"), sem("rms_made"), sem("q_norm_made"), sem("q_root_made")
        s_shift, s_exp, s_weight = sem("logits_shifted"), sem("exp_made"), sem("weights_made")
        s_qhat = sem("q_normalized")
        s_pick = sem("picks_made")
        s_rank = sem("ranks_done")
        s_dve = sem("router_steps")
        s_slot, s_lane_hot, s_tile_is, s_tile_hot = (sem("slots_made"), sem("lanes_one_hot"), sem("tiles_compared"),
                                                     sem("tiles_one_hot"))
        s_inv = sem("slots_inverted")
        s_tables, s_row = sem("tables_made"), sem("tile_rows_made")
        s_rot = sem("rotation_made")
        s_w3tp, s_w3t = sem("w3_transposed"), sem("w3_t_copied")
        s_w3rp, s_w3r = sem("w3_rotated"), sem("w3_rot_copied")
        s_b3tp, s_b3t, s_b3rp, s_b3r = sem("b3_transposed"), sem("b3_spread"), sem("b3_rotated"), sem("b3_rows_copied")
        s_xrp, s_base = sem("x_rotated"), sem("base_copied")
        s_gather = [sem(f"gathered{n}") for n in range(UNROLL)]
        s_t0, s_xgt = sem("tile_transposed"), sem("tile_t_copied")
        s_l1, s_h1, s_t1, s_h1t = sem("layer1_done"), sem("h1_biased"), sem("h1_transposed"), sem("h1_t_ready")
        s_l2, s_h2, s_t2, s_h2t = sem("layer2_done"), sem("h2_biased"), sem("h2_transposed"), sem("h2_t_ready")
        s_l3, s_y = sem("layer3_done"), sem("y_ready")
        s_scatter = [sem(f"scattered{n}") for n in range(UNROLL)]
        s_back = [sem(f"y_loaded{g}") for g in range(CHUNKS)]
        s_scaled, s_partial, s_out, s_store = sem("second_scaled"), sem("partial_made"), sem("out_made"), sem("stored")

        block = ctx.enter_context(nc.Block())

        x_rows = x.rearrange("b s h -> (b s) h")
        x_pc = x_rows.rearrange("(p c) h -> p c h", c=COLS)
        out_pc = out.rearrange("b s h -> (b s) h").rearrange("(p c) h -> p c h", c=COLS)

        def chunk(g):
            return slice(g * CPC, (g + 1) * CPC)

        @block.sync
        def _(sp):
            def load_x(n):
                part = slice(n * COLS // X_LOADS, (n + 1) * COLS // X_LOADS)
                sp.dma_start(x_sb[:, part, :], x_pc[:, part, :]).then_inc(s_x[n], 16)

            load_x(0)
            sp.dma_start(wg_sb[:, :], wg_w).then_inc(s_router_in, 16)
            sp.dma_start(rms_sb[:, :], rms_w.rearrange("(h a) -> h a", a=1)).then_inc(s_router_in, 16)
            load_x(1)
            sp.dma_start(gg_sb[:, :], gg_w).then_inc(s_bias_in, 16)
            sp.dma_start(gate_b_sb[:, 0, :], wg_b.rearrange("(a e) -> a e", a=1)).then_inc(s_bias_in, 16)
            sp.dma_start(gate_b_sb[:, 1, :], gg_b.rearrange("(a e) -> a e", a=1)).then_inc(s_bias_in, 16)
            sp.dma_start(b3_sb[:, :], b3).then_inc(s_b3_in, 16)
            sp.dma_start(w3_sb[:, :, :], w3.rearrange("e (c p) h -> p (e c) h", p=P)).then_inc(s_w3, 16)
            sp.dma_start(w1_sb[:, :].rearrange("p (e m) -> p e m", e=E), w1.rearrange("e h m -> h e m")).then_inc(s_w1, 16)
            sp.dma_start(b1_rows[:, :].rearrange("p (e m) -> p e m", e=E), b1.rearrange("(a e) m -> a e m", a=1).to_broadcast([P, E, M])).then_inc(s_b1, 16)
            for c in range(MC):
                sp.dma_start(w2_sb[:, c * E * M:(c + 1) * E * M].rearrange("p (e m) -> p e m", e=E),
                             w2[:, c * P:(c + 1) * P, :].rearrange("e p m -> p e m")).then_inc(s_w2, 16)
            sp.dma_start(b2_rows[:, :].rearrange("p (e m) -> p e m", e=E), b2.rearrange("(a e) m -> a e m", a=1).to_broadcast([P, E, M])).then_inc(s_b2, 16)
            for n in range(UNROLL):
                sp.wait_ge(s_scatter[n], 16 * len(range(n, NUM_TILES, UNROLL)))
            y_pc = y_rows[0:TOP_K * TOKENS, :].rearrange("(k p c) h -> p k c h", k=TOP_K, c=COLS)
            for g in range(CHUNKS):
                for k in range(TOP_K):
                    sp.dma_start(y_back[:, k, chunk(g), :], y_pc[:, k, chunk(g), :]).then_inc(s_back[g], 16)
            for g in range(CHUNKS):
                sp.wait_ge(s_out, g + 1)
                sp.dma_start(out_pc[:, chunk(g), :], out_sb[:, chunk(g), :]).then_inc(s_store, 16)
            sp.wait_ge(s_store, 16 * CHUNKS)

        @block.gpsimd
        def _(pool):
            pool.memset(ident[:, :], 0.0).then_inc(s_pool, 1)
            pool.wait_ge(s_pool, 1)
            pool.affine_select(out=ident[:, :], in_=ident[:, :], compare_op=ALU.not_equal, fill=1.0,
                               base=0, pattern=[[-1, P]], channel_multiplier=1).then_inc(s_const, 1)
            pool.wait_ge(s_quat_in, 16 * 3)
            pool.tensor_copy(cond_rep[:, :, :], cond_t[:, :].unsqueeze(2).to_broadcast([G, BATCH, COLS]))
            pool.memset(ones_row[:, :], 1.0).then_inc(s_const, 1)
            pool.iota(rev_e_i[:, :], pattern=[[-1, E]], base=E, channel_multiplier=0).then_inc(s_pool, 1)
            pool.memset(before[:, :], 1.0).then_inc(s_pool, 1)
            pool.wait_ge(s_pool, 2)
            pool.tensor_copy(rev_e[:, :], rev_e_i[:, :]).then_inc(s_const, 1)
            pool.wait_ge(s_qhat, 2)
            for i in range(QUAT):
                for k in range(QUAT):
                    a, sign = LEFT[i][k]
                    pool.tensor_scalar(left[:, i, k:k + 1], ql_n[:, a:a + 1], float(sign), None, ALU.mult)
                    a, sign = RIGHT_CONJ[k][i]
                    last = pool.tensor_scalar(right_t[:, i, k:k + 1], qr_n[:, a:a + 1], float(sign), None,
                                              ALU.mult)
            last.then_inc(s_coefs, 1)
            pool.wait_ge(s_pool, 3)
            pool.affine_select(out=before[:, :], in_=before[:, :], compare_op=ALU.is_ge, fill=0.0,
                               base=-1, pattern=[[1, P]], channel_multiplier=-1)
            pool.memset(ones16[:, :], 1.0)
            pool.memset(minus16[:, :], -1.0)
            pool.memset(zeros16[:, :], 0.0)
            pool.memset(zeros_e[:, :], 0.0)
            pool.memset(picks_before[:, 0:1], 0.0)
            pool.iota(lane_i[:, :], pattern=[[1, P]], base=0, channel_multiplier=0)
            pool.iota(thresh_i[:, :], pattern=[[P, COLS]], base=0, channel_multiplier=0)
            pool.iota(token1_i[:, :], pattern=[[1, COLS]], base=1, channel_multiplier=COLS)
            pool.iota(tiles_i[:, :, :], pattern=[[UNROLL, ROWS], [1, ROW]], base=-1, channel_multiplier=0)
            pool.iota(spare_i[:, :], pattern=[[P, TABLE]], base=TOP_K * TOKENS + 1,
                      channel_multiplier=1).then_inc(s_pool, 1)
            pool.wait_ge(s_pool, 4)
            pool.tensor_copy(lane16[:, :], lane_i[:, :])
            pool.tensor_copy(thresh[:, :], thresh_i[:, :])
            pool.tensor_copy(token1[:, :], token1_i[:, :])
            pool.tensor_copy(tiles_f[:, :, :], tiles_i[:, :, :])
            pool.tensor_copy(spare[:, :], spare_i[:, :]).then_inc(s_const, 1)
            for k in range(TOP_K):
                pairs = slice(k * COLS, (k + 1) * COLS)
                pool.wait_ge(s_tile_is, k + 1)
                pool.tensor_tensor(tile_hot[:, pairs, :], tile_is[:, pairs, :],
                                   token1[:, :].unsqueeze(2).to_broadcast([P, COLS, TABLE]),
                                   ALU.mult).then_inc(s_tile_hot, 1)

            def gather(t):
                wait_count(pool, s_t0, t - UNROLL + 1)
                pool.indirect_dma_start(
                    out=x_g[:, t % UNROLL, :], out_offset=None, in_=x_rows,
                    in_offset=bass.IndirectOffsetOnAxis(ap=gather_row[:, t:t + 1], axis=0),
                ).then_inc(s_gather[t % UNROLL], 16)

            def scatter(t):
                pool.wait_ge(s_y, t + 1)
                pool.indirect_dma_start(
                    out=y_rows, out_offset=bass.IndirectOffsetOnAxis(ap=scatter_row[:, t:t + 1], axis=0),
                    in_=y[:, t % UNROLL, :], in_offset=None,
                ).then_inc(s_scatter[t % UNROLL], 16)

            pool.wait_ge(s_tables, 1)
            for t in range(NUM_TILES + GATHERS_AHEAD):
                if t < NUM_TILES:
                    gather(t)
                if t == 0:
                    pool.wait_ge(s_tables, 3)
                if t >= GATHERS_AHEAD:
                    scatter(t - GATHERS_AHEAD)

        @block.scalar
        def _(act):
            act.dma_start(cond_t[:, :], cond.rearrange("b g -> g b"),
                          allow_slow_non_contiguous=True).then_inc(s_quat_in, 16)
            act.dma_start(qr_t[:, :], q_right.rearrange("q d -> d q"),
                          allow_slow_non_contiguous=True).then_inc(s_quat_in, 16)
            act.dma_start(gate_t[:, :], gate.rearrange("a b c d -> d (a b c)")).then_inc(s_quat_in, 16)
            for g in range(CHUNKS):
                act.wait_ge(s_x[g * X_LOADS // CHUNKS], 16)
                act.activation(x_sq[:, chunk(g), :], x_sb[:, chunk(g), :], ACT.Square).then_inc(s_sq, 1)
                act.wait_ge(s_tr, g + 1)
                act.activation(x_t[:, chunk(g), :], bank[g % 2][:, :], ACT.Copy).then_inc(s_xt, 1)
                if g == 0:
                    act.wait_ge(s_qn, 1)
                    act.activation(q_root[:, :], q_norm[:, :], ACT.Sqrt).then_inc(s_qroot, 1)
            act.wait_ge(s_var, 1)
            act.activation(rms[:, :], var[:, :], ACT.Sqrt).then_inc(s_rms, 1)
            for g in range(CHUNKS):
                act.wait_ge(s_w3tp, g + 1)
                act.activation(w3_t[:, chunk(g), :], bank[6 + g % 2][:, :], ACT.Copy).then_inc(s_w3t, 1)
            for g in range(CHUNKS):
                act.wait_ge(s_w3rp, g + 1)
                act.activation(w3_rot[:, g * 512:(g + 1) * 512], bank[6 + g % 2][:, :], ACT.Copy).then_inc(s_w3r, 1)
            act.wait_ge(s_b3tp, 1)
            act.activation(b3_t[:, :], bank[1][:, 0:E], ACT.Copy).then_inc(s_b3t, 1)
            act.wait_ge(s_b3t, 1)
            act.activation(b3_cols[:, :, :], b3_t[:, :].unsqueeze(2).to_broadcast([H, E, P]),
                           ACT.Copy).then_inc(s_b3t, 1)
            for g in range(2):
                act.wait_ge(s_b3rp, g + 1)
                act.activation(b3_rows[:, 4 * g:4 * g + 4, 0, :], bank[6 + g % 2][:, :].rearrange("p (e h) -> p e h", h=H),
                               ACT.Copy).then_inc(s_b3r, 1)
            for g in range(CHUNKS):
                act.wait_ge(s_xrp, g + 1)
                act.activation(base[:, chunk(g), :], bank[6 + g % 2][:, :], ACT.Copy).then_inc(s_base, 1)

            act.wait_ge(s_shift, 2)
            act.activation(expv[:, :, :], shifted[:, :, :], ACT.Exp)
            act.activation(exp_best[:, :, :], shifted_best[:, :, :], ACT.Exp).then_inc(s_exp, 1)

            def copy_tile_t(t):
                act.wait_ge(s_t0, t + 1)
                act.activation(x_gt[:, :], bank[0][:, 0:P], ACT.Copy).then_inc(s_xgt, 1)

            def relu1(t):
                act.wait_ge(s_t1, t + 1)
                act.activation(h1_t[:, :, :], bank[2][:, 0:M], ACT.Relu).then_inc(s_h1t, 1)

            def relu2(t):
                act.wait_ge(s_t2, t + 1)
                act.activation(h2_t[:, :, :], bank[4][:, 0:M], ACT.Relu).then_inc(s_h2t, 1)

            def peeled(i):
                if 0 <= i + 1 < NUM_TILES:
                    relu1(i + 1)
                if i + 2 < NUM_TILES:
                    copy_tile_t(i + 2)
                if 0 <= i < NUM_TILES:
                    relu2(i)

            for i in range(-2, FIRST_STEADY):
                peeled(i)
            with act.Fori(0, STEADY_TRIPS) as n:
                for u in range(UNROLL):
                    i = n * UNROLL + (FIRST_STEADY + u)
                    relu1(i + 1)
                    copy_tile_t(i + 2)
                    relu2(i)
            for i in range(PEEL_AFTER, LAST_STEP + 1):
                peeled(i)

            act.wait_ge(s_weight, 1)
            for g in range(CHUNKS):
                act.wait_ge(s_back[g], 16 * TOP_K)
                for c in range(g * CPC, (g + 1) * CPC):
                    last = act.activation(scaled[:, c, :], y_back[:, 1, c, :], ACT.Copy,
                                          scale=weight[:, 1, c:c + 1])
                last.then_inc(s_scaled, 1)

        @block.vector
        def _(dve):
            steps = [0]

            def step(instruction):
                steps[0] += 1
                instruction.then_inc(s_dve, 1)
                dve.wait_ge(s_dve, steps[0])

            def over_e(ap):
                return ap.unsqueeze(2).to_broadcast([P, COLS, E])

            dve.wait_ge(s_quat_in, 16 * 3)
            dve.tensor_tensor(q_sq[:, 0:BATCH], cond_t[:, :], cond_t[:, :], ALU.mult)
            step(dve.tensor_tensor(q_sq[:, BATCH:], qr_t[:, :], qr_t[:, :], ALU.mult))
            dve.tensor_reduce(q_norm[:, 0:1], q_sq[:, 0:BATCH], X_AXIS, ALU.add)
            step(dve.tensor_reduce(q_norm[:, 1:2], q_sq[:, BATCH:], X_AXIS, ALU.add))
            dve.tensor_scalar(q_norm[:, :], q_norm[:, :], EPS_QUAT, None, ALU.add).then_inc(s_qn, 1)
            dve.wait_ge(s_router_in, 16 * 2)
            dve.tensor_scalar(wg_rms[:, :], wg_sb[:, :], rms_sb[:, :], None, ALU.mult).then_inc(s_wgr, 1)
            for g in range(CHUNKS):
                dve.wait_ge(s_sq, g + 1)
                last = dve.tensor_reduce(var[:, chunk(g)], x_sq[:, chunk(g), :], X_AXIS, ALU.add)
                if g == 0:
                    dve.wait_ge(s_qroot, 1)
                    step(dve.reciprocal(q_inv[:, :], q_root[:, :]))
                    dve.tensor_scalar(ql_n[:, :], cond_t[:, 0:QUAT], q_inv[:, 0:1], None,
                                      ALU.mult).then_inc(s_qhat, 1)
                    dve.tensor_scalar(qr_n[:, :], qr_t[:, :], q_inv[:, 1:2], gate_t[:, :], ALU.mult,
                                      ALU.mult).then_inc(s_qhat, 1)
            step(last)
            dve.tensor_scalar(var[:, :], var[:, :], 1.0 / H, EPS_RMS, ALU.mult, ALU.add).then_inc(s_var, 1)
            dve.wait_ge(s_rms, 1)
            step(dve.reciprocal(rstd[:, :], rms[:, :]))

            dve.wait_ge(s_logit, 1)
            step(dve.tensor_tensor(logits[:, :, :], bank[2][:, 0:P].rearrange("p (c e) -> p c e", e=E),
                                   over_e(rstd[:, :]), ALU.mult))
            dve.wait_ge(s_bias, 1)
            step(dve.tensor_tensor(logits[:, :, :], logits[:, :, :],
                                   bank[3][:, 0:E].unsqueeze(1).to_broadcast([P, COLS, E]), ALU.add))
            dve.wait_ge(s_const, 3)
            rev = rev_e[:, :].unsqueeze(1).to_broadcast([P, COLS, E])
            for k, source in enumerate((logits, rest)):
                step(dve.tensor_reduce(best[:, k, :], source[:, :, :], X_AXIS, ALU.max))
                step(dve.tensor_tensor(key[:, :, :], source[:, :, :], over_e(best[:, k, :]), ALU.is_equal))
                step(dve.tensor_tensor(key[:, :, :], key[:, :, :], rev, ALU.mult))
                step(dve.tensor_reduce(key_max[:, :], key[:, :, :], X_AXIS, ALU.max))
                step(dve.tensor_tensor(chosen[:, k, :, :], rev, over_e(key_max[:, :]), ALU.is_equal))
                if k == 0:
                    step(dve.scalar_tensor_tensor(out=rest[:, :, :], in0=chosen[:, 0, :, :], scalar=MASK,
                                                  in1=logits[:, :, :], op0=ALU.mult, op1=ALU.add))
            step(dve.tensor_tensor(picks[:, :, :].rearrange("p e c -> p c e"), chosen[:, 0, :, :],
                                   chosen[:, 1, :, :], ALU.add))
            dve.wait_ge(s_const, 4)
            dve.tensor_tensor_scan(picks_before[:, 1:], picks[:, :, :].rearrange("p e c -> p (e c)"),
                                   zeros16[:, :], 0.0, ALU.add, ALU.add).then_inc(s_pick, 1)
            dve.wait_ge(s_coefs, 1)
            step(dve.tensor_tensor(lr_prod[:, :, :, :], left[:, :, :].unsqueeze(1).to_broadcast([QD, QUAT, QUAT, QUAT]),
                                   right_t[:, :, :].unsqueeze(2).to_broadcast([QD, QUAT, QUAT, QUAT]), ALU.mult))
            step(dve.tensor_reduce(coef[:, :, :], lr_prod[:, :, :, :], X_AXIS, ALU.add))
            for j in range(QUAT):
                last = dve.tensor_tensor(rot0[QD * j:QD * (j + 1), :].rearrange("p (i d) -> p i d", i=QUAT),
                                         ident[0:QD, 0:QD].unsqueeze(1).to_broadcast([QD, QUAT, QD]),
                                         coef[:, j, :].unsqueeze(2).to_broadcast([QD, QUAT, QD]), ALU.mult)
            step(last)
            dve.tensor_tensor(rot[:, :], rot0[:, :], ident[:, :], ALU.add).then_inc(s_rot, 1)
            dve.wait_ge(s_rank, 1)
            step(dve.tensor_tensor(over[:, :, :], bank[4][:, 0:E].unsqueeze(2).to_broadcast([P, E, COLS]),
                                   thresh[:, :].unsqueeze(1).to_broadcast([P, E, COLS]), ALU.is_gt))
            step(dve.tensor_reduce(tile_count[:, :], over[:, :, :], X_AXIS, ALU.add))
            step(dve.tensor_tensor_scan(tile_end[:, :], tile_count[:, :], zeros_e[:, :], 0.0, ALU.add, ALU.add))
            step(dve.tensor_tensor(tile_start[:, :], tile_end[:, :], tile_count[:, :], ALU.subtract))
            step(dve.scalar_tensor_tensor(
                out=position[:, :, :], in0=tile_start[:, :].unsqueeze(2).to_broadcast([P, E, COLS]),
                scalar=float(P), in1=bank[5][:, 0:P].rearrange("p (e c) -> p e c", e=E),
                op0=ALU.mult, op1=ALU.add))
            for k in range(TOP_K):
                last = dve.tensor_tensor(pos_chosen[:, k, :, :], chosen[:, k, :, :],
                                         position[:, :, :].rearrange("p e c -> p c e"), ALU.mult)
            step(last)
            step(dve.tensor_reduce(slot_i[:, :], pos_chosen[:, :, :, :].rearrange("p k c e -> p (k c) e"),
                                   X_AXIS, ALU.max))
            dve.tensor_scalar(tile_of_i[:, :], slot_i[:, :], 7, None, ALU.arith_shift_right).then_inc(s_slot, 1)
            dve.tensor_scalar(lane_of_i[:, :], slot_i[:, :], P - 1, None, ALU.bitwise_and).then_inc(s_slot, 1)
            dve.wait_ge(s_slot, 2)
            for k in range(TOP_K):
                pairs = slice(k * COLS, (k + 1) * COLS)
                dve.tensor_tensor(tile_is[:, pairs, :],
                                  lane16[:, 0:TABLE].unsqueeze(1).to_broadcast([P, COLS, TABLE]),
                                  tile_of_i[:, pairs].unsqueeze(2).to_broadcast([P, COLS, TABLE]),
                                  ALU.is_equal).then_inc(s_tile_is, 1)
            for n in range(HOT_PARTS):
                pairs = slice(n * PAIRS // HOT_PARTS, (n + 1) * PAIRS // HOT_PARTS)
                shape = [P, PAIRS // HOT_PARTS, P]
                dve.tensor_tensor(lane_hot[:, pairs, :], lane16[:, :].unsqueeze(1).to_broadcast(shape),
                                  lane_of_i[:, pairs].unsqueeze(2).to_broadcast(shape),
                                  ALU.is_equal).then_inc(s_lane_hot, 1)
            dve.tensor_tensor(ended[:, :, :], tiles_f[:, :, :].rearrange("a r k -> a (r k)").unsqueeze(2).to_broadcast([1, ROWS * ROW, E]),
                              tile_end[0:1, :].unsqueeze(1).to_broadcast([1, ROWS * ROW, E]), ALU.is_ge).then_inc(s_dve, 1)
            steps[0] += 1
            dve.wait_ge(s_dve, steps[0])
            step(dve.tensor_reduce(expert_f[:, :], ended[:, :, :], X_AXIS, ALU.add))
            dve.tensor_scalar(tile_row[:, :, :].rearrange("a r k -> a (r k)"), expert_f[:, :], float(E - 1), float(M),
                              ALU.min, ALU.mult).then_inc(s_row, 1)
            dve.wait_ge(s_inv, 1)
            step(dve.tensor_copy(second[:, :], bank[3][:, 0:TABLE]))
            step(dve.tensor_tensor(filled[:, :], bank[2][:, 0:TABLE], second[:, :], ALU.add))
            dve.tensor_scalar(gather_row[:, :], filled[:, :], -1.0, 0.0, ALU.add, ALU.max).then_inc(s_tables, 1)
            dve.tensor_scalar(is_second[:, :], second[:, :], 0.0, float(TOKENS), ALU.is_gt, ALU.mult)
            step(dve.scalar_tensor_tensor(out=is_unused[:, :], in0=filled[:, :], scalar=0.0, in1=spare[:, :],
                                          op0=ALU.is_equal, op1=ALU.mult))
            dve.tensor_tensor(row_1[:, :], filled[:, :], is_second[:, :], ALU.add).then_inc(s_tables, 1)
            dve.wait_ge(s_tables, 2)
            dve.scalar_tensor_tensor(out=scatter_row[:, :], in0=row_1[:, :], scalar=-1.0, in1=is_unused[:, :],
                                     op0=ALU.add, op1=ALU.add).then_inc(s_tables, 1)
            dve.tensor_tensor(shifted_best[:, :, :], best[:, :, :],
                              best[:, 0, :].unsqueeze(1).to_broadcast([P, TOP_K, COLS]),
                              ALU.subtract).then_inc(s_shift, 1)
            dve.tensor_tensor(shifted[:, :, :], logits[:, :, :], over_e(best[:, 0, :]),
                              ALU.subtract).then_inc(s_shift, 1)
            dve.wait_ge(s_exp, 1)
            step(dve.tensor_reduce(row_sum[:, :], expv[:, :, :], X_AXIS, ALU.add))
            step(dve.reciprocal(row_sum[:, :], row_sum[:, :]))
            dve.tensor_tensor(weight[:, :, :], exp_best[:, :, :],
                              row_sum[:, :].unsqueeze(1).to_broadcast([P, TOP_K, COLS]),
                              ALU.mult).then_inc(s_weight, 1)

            def bias1(t, e):
                dve.wait_ge(s_l1, t + 1)
                dve.tensor_tensor(h1[:, :], bank[1][:, 0:M], b1_rows[:, bass.ds(e, M)], ALU.add).then_inc(s_h1, 1)

            def bias2(t, e):
                dve.wait_ge(s_l2, t + 1)
                dve.tensor_tensor(h2[:, :], bank[3][:, 0:M], b2_rows[:, bass.ds(e, M)], ALU.add).then_inc(s_h2, 1)

            def bias3(t, e, slot_n, round_n):
                dve.wait_ge(s_l3, t + 1)
                wait_count(dve, s_scatter[slot_n], 16 * round_n)
                dve.tensor_tensor(y[:, slot_n, :], bank[5][:, 0:H], b3_rows[:, :, :, :].rearrange("p e a h -> p (e a h)")[:, bass.ds(e, H)], ALU.add).then_inc(s_y, 1)


            def peeled(i, experts):
                if 0 <= i + 1 < NUM_TILES:
                    bias1(i + 1, experts[i + 1])
                if 0 <= i < NUM_TILES:
                    bias2(i, experts[i])
                if 0 <= i - 1 < NUM_TILES:
                    bias3(i - 1, experts[i - 1], (i - 1) % UNROLL, (i - 1) // UNROLL)

            dve.wait_ge(s_row, 1)
            dve.wait_ge(s_b1, 16)
            dve.wait_ge(s_b2, 16)
            dve.wait_ge(s_b3r, 2)
            early, live, ahead = expert_registers(dve)
            dve.reg_load(early, tile_row[0:1, 0:EARLY_ROWS, :].rearrange("a r k -> a (r k)"))
            experts = {UNROLL * (k // ROW) - 1 + k % ROW: as_expert(dve, early[k]) for k in range(1, len(early))}
            for i in range(-2, FIRST_STEADY):
                peeled(i, experts)
            for k in range(LIVE):
                dve.reg_mov(live[k], experts[FIRST_STEADY - 1 + k])
            with dve.Fori(0, STEADY_TRIPS) as n:
                first = n * UNROLL + FIRST_STEADY
                experts = [as_expert(dve, r) for r in live]
                for u in range(UNROLL):
                    i = first + u
                    bias1(i + 1, experts[u + 2])
                    bias2(i, experts[u + 1])
                    bias3(i - 1, experts[u], u, n + (FIRST_STEADY - 1) // UNROLL)
                    if u == 1:
                        load_ahead(dve, ahead, tile_row, n)
                next_trip(dve, live, ahead)
            experts = {PEEL_AFTER - 1 + k: as_expert(dve, live[k]) for k in range(3)}
            for i in range(PEEL_AFTER, LAST_STEP + 1):
                peeled(i, experts)

            dve.wait_ge(s_base, CHUNKS)
            dve.wait_ge(s_weight, 1)
            for g in range(CHUNKS):
                dve.wait_ge(s_back[g], 16 * TOP_K)
                for c in range(g * CPC, (g + 1) * CPC):
                    last = dve.scalar_tensor_tensor(out=partial[:, c, :], in0=y_back[:, 0, c, :],
                                                    scalar=weight[:, 0, c:c + 1], in1=base[:, c, :],
                                                    op0=ALU.mult, op1=ALU.add)
                last.then_inc(s_partial, 1)
                dve.wait_ge(s_partial, g + 1)
                dve.wait_ge(s_scaled, g + 1)
                dve.tensor_tensor(out_sb[:, chunk(g), :], partial[:, chunk(g), :], scaled[:, chunk(g), :],
                                  ALU.add).then_inc(s_out, 1)

        @block.tensor
        def _(pe):
            def transpose_x(g):
                pe.wait_ge(s_x[g * X_LOADS // CHUNKS], 16)
                wait_count(pe, s_xt, g - 1)
                for j in range(CPC):
                    last = pe.transpose(bank[g % 2][:, j * P:(j + 1) * P], x_sb[:, g * CPC + j, :], ident[:, :])
                last.then_inc(s_tr, 1)

            def gate_logits(g):
                pe.wait_ge(s_xt, g + 1)
                for c in range(g * CPC, (g + 1) * CPC):
                    last = pe.matmul(bank[2][:, c * E:(c + 1) * E], x_t[:, c, :], wg_rms[:, :],
                                     start=True, stop=True)
                return last

            pe.wait_ge(s_const, 1)
            transpose_x(0)
            transpose_x(1)
            pe.wait_ge(s_wgr, 1)
            gate_logits(0)
            transpose_x(2)
            gate_logits(1)
            transpose_x(3)
            gate_logits(2)
            gate_logits(3).then_inc(s_logit, 1)
            pe.wait_ge(s_bias_in, 16 * 3)
            pe.wait_ge(s_const, 2)
            pe.matmul(bank[3][:, 0:E], cond_rep[:, :, :].rearrange("g b c -> g (b c)"), gg_sb[:, :],
                      start=True, stop=False)
            pe.matmul(bank[3][:, 0:E], ones_row[:, :], gate_b_sb[:, 0, :], start=False, stop=False)
            pe.matmul(bank[3][:, 0:E], ones_row[:, :], gate_b_sb[:, 1, :], start=False, stop=True).then_inc(s_bias, 1)
            pe.wait_ge(s_w3, 16)
            for g in range(CHUNKS):
                wait_count(pe, s_w3t, g - 1)
                for j in range(CPC):
                    last = pe.transpose(bank[6 + g % 2][:, j * P:(j + 1) * P], w3_sb[:, g * CPC + j, :], ident[:, :])
                last.then_inc(s_w3tp, 1)
            pe.wait_ge(s_b3_in, 16)
            pe.transpose(bank[1][:, 0:E], b3_sb[:, :], ident[0:E, 0:E]).then_inc(s_b3tp, 1)
            pe.wait_ge(s_const, 4)
            pe.wait_ge(s_pick, 1)
            at_start = picks_before[:, 0:E * COLS:COLS]
            pe.matmul(bank[5][:, 0:P], before[:, :], picks[:, :, :].rearrange("p e c -> p (e c)"),
                      start=True, stop=False)
            pe.matmul(bank[5][:, 0:P], ones16[:, :], picks_before[:, 0:E * COLS], start=False, stop=False)
            pe.matmul(bank[5][:, 0:P].rearrange("p (e c) -> p e c", e=E), minus16[:, :],
                      at_start.unsqueeze(2).to_broadcast([P, E, COLS]), start=False, stop=True)
            pe.matmul(bank[4][:, 0:E], ones16[:, :], picks_before[:, COLS::COLS], start=True, stop=False)
            pe.matmul(bank[4][:, 0:E], minus16[:, :], at_start, start=False, stop=True).then_inc(s_rank, 1)
            pe.wait_ge(s_rot, 1)
            for g in range(CHUNKS):
                pe.wait_ge(s_w3t, CHUNKS)
                wait_count(pe, s_w3r, g - 1)
                for j in range(CPC):
                    last = pe.matmul(bank[6 + g % 2][:, j * P:(j + 1) * P], w3_t[:, g * CPC + j, :], rot[:, :],
                                     start=True, stop=True)
                last.then_inc(s_w3rp, 1)
            for n in range(PAIRS):
                if n % (PAIRS // HOT_PARTS) == 0:
                    pe.wait_ge(s_lane_hot, n * HOT_PARTS // PAIRS + 1)
                if n % COLS == 0:
                    pe.wait_ge(s_tile_hot, n // COLS + 1)
                last = pe.matmul(bank[2 + n // COLS][:, 0:TABLE], lane_hot[:, n, :], tile_hot[:, n, :],
                                 start=n % COLS == 0, stop=n % COLS == COLS - 1)
            last.then_inc(s_inv, 1)
            pe.wait_ge(s_b3t, 2)
            for g in range(2):
                pe.wait_ge(s_w3r, 3 + g)
                for j in range(4):
                    last = pe.matmul(bank[6 + g][:, j * H:(j + 1) * H], b3_cols[:, 4 * g + j, :], rot[:, :],
                                     start=True, stop=True)
                last.then_inc(s_b3rp, 1)
            for g in range(CHUNKS):
                pe.wait_ge(s_b3r, min(g + 1, 2))
                wait_count(pe, s_base, g - 1)
                for j in range(CPC):
                    last = pe.matmul(bank[6 + g % 2][:, j * H:(j + 1) * H], x_t[:, g * CPC + j, :], rot[:, :],
                                     start=True, stop=True)
                last.then_inc(s_xrp, 1)

            def transpose_tile(t, slot_n, round_n):
                pe.wait_ge(s_gather[slot_n], 16 * (round_n + 1))
                pe.transpose(bank[0][:, 0:P], x_g[:, slot_n, :], ident[:, :]).then_inc(s_t0, 1)

            def layer1(t, e):
                pe.wait_ge(s_xgt, t + 1)
                pe.matmul(bank[1][:, 0:M], x_gt[:, :], w1_sb[:, bass.ds(e, M)], start=True, stop=True).then_inc(s_l1, 1)

            def transpose_h1(t):
                pe.wait_ge(s_h1, t + 1)
                for c in range(MC):
                    last = pe.transpose(bank[2][:, c * P:(c + 1) * P], h1[:, c * P:(c + 1) * P], ident[:, :])
                last.then_inc(s_t1, 1)

            def layer2(t, e):
                pe.wait_ge(s_h1t, t + 1)
                for c in range(MC):
                    last = pe.matmul(bank[3][:, 0:M], h1_t[:, c, :],
                                     w2_sb[:, bass.ds(e + c * E * M, M)],
                                     start=c == 0, stop=c == MC - 1)
                last.then_inc(s_l2, 1)

            def transpose_h2(t):
                pe.wait_ge(s_h2, t + 1)
                for c in range(MC):
                    last = pe.transpose(bank[4][:, c * P:(c + 1) * P], h2[:, c * P:(c + 1) * P], ident[:, :])
                last.then_inc(s_t2, 1)

            def layer3(t, e):
                pe.wait_ge(s_h2t, t + 1)
                wait_count(pe, s_y, t)
                for c in range(MC):
                    last = pe.matmul(bank[5][:, 0:H], h2_t[:, c, :],
                                     w3_rot[:, bass.ds(e + c * H, H)],
                                     start=c == 0, stop=c == MC - 1)
                last.then_inc(s_l3, 1)


            def peeled(i, experts):
                if 0 <= i + 1 < NUM_TILES:
                    layer1(i + 1, experts[i + 1])
                if 0 <= i < NUM_TILES:
                    layer2(i, experts[i])
                if 0 <= i + 1 < NUM_TILES:
                    transpose_h1(i + 1)
                if i + 2 < NUM_TILES:
                    transpose_tile(i + 2, (i + 2) % UNROLL, (i + 2) // UNROLL)
                if 0 <= i - 1 < NUM_TILES:
                    layer3(i - 1, experts[i - 1])
                if 0 <= i < NUM_TILES:
                    transpose_h2(i)

            pe.wait_ge(s_row, 1)
            pe.wait_ge(s_w1, 16)
            pe.wait_ge(s_w2, 16 * MC)
            pe.wait_ge(s_w3r, CHUNKS)
            early, live, ahead = expert_registers(pe)
            pe.reg_load(early, tile_row[0:1, 0:EARLY_ROWS, :].rearrange("a r k -> a (r k)"))
            experts = {UNROLL * (k // ROW) - 1 + k % ROW: as_expert(pe, early[k]) for k in range(1, len(early))}
            for i in range(-2, FIRST_STEADY):
                peeled(i, experts)
            for k in range(LIVE):
                pe.reg_mov(live[k], experts[FIRST_STEADY - 1 + k])
            with pe.Fori(0, STEADY_TRIPS) as n:
                first = n * UNROLL + FIRST_STEADY
                experts = [as_expert(pe, r) for r in live]
                for u in range(UNROLL):
                    i = first + u
                    layer1(i + 1, experts[u + 2])
                    layer2(i, experts[u + 1])
                    if u == 1:
                        load_ahead(pe, ahead, tile_row, n)
                    transpose_h1(i + 1)
                    transpose_tile(i + 2, u, n + (FIRST_STEADY + 2) // UNROLL)
                    layer3(i - 1, experts[u])
                    transpose_h2(i)
                next_trip(pe, live, ahead)
            experts = {PEEL_AFTER - 1 + k: as_expert(pe, live[k]) for k in range(3)}
            for i in range(PEEL_AFTER, LAST_STEP + 1):
                peeled(i, experts)


def expert_registers(engine):
    return [[engine.alloc_register(f"{name}{k}") for k in range(count)]
            for name, count in (("early", EARLY_ROWS * ROW), ("live", LIVE), ("ahead", ROW))]


def as_expert(engine, register):
    return engine.snap(register, min_val=0, max_val=(E - 1) * M)


def load_ahead(engine, ahead, tile_row, n):
    row = n + ((FIRST_STEADY + 2) // UNROLL + 1)
    engine.reg_load(ahead, tile_row[0:1, bass.ds(row, 1), :].rearrange("a r k -> a (r k)"))


def next_trip(engine, live, ahead):
    engine.reg_mov(live[0], live[UNROLL])
    engine.reg_mov(live[1], live[UNROLL + 1])
    for k in range(UNROLL):
        engine.reg_mov(live[2 + k], ahead[k])


INPUTS = ["x", "cond_256", "L0_cond_rms_w", "L0_cond_wg_W", "L0_cond_wg_b", "L0_cond_gg_W", "L0_cond_gg_b",
          "L0_cond_W1", "L0_cond_b1", "L0_cond_W2", "L0_cond_b2", "L0_cond_W3", "L0_cond_b3",
          "L1_cond_q_right", "L1_cond_spectral_gate"]


def kernel(**inputs):
    import numpy as np
    import concourse.bacc as bacc
    from concourse.bass_utils import run_bass_kernel_spmd

    nc = bacc.Bacc("TRN2", target_bir_lowering=False, num_devices=1)
    arrays, args = {}, []
    for name in INPUTS:
        a = np.ascontiguousarray(inputs[name])
        arrays[f"in_{name}"] = a
        args.append(nc.dram_tensor(f"in_{name}", a.shape, mybir.dt.from_np(a.dtype), kind="ExternalInput").ap())
    out = nc.dram_tensor("out_rotated", (BATCH, SEQ, H), F32, kind="ExternalOutput").ap()
    moe_rotation(nc, *args, out)
    result = run_bass_kernel_spmd(nc, [arrays], core_ids=[0])
    return result.results[0]["out_rotated"]
```
